# Optimizing a Trainium2 kernel written in Bass

```python
import numpy as np
import jax
import jax.numpy as jnp

def _softmax(x, axis=-1):
    return jax.nn.softmax(x, axis=axis)

def _gelu(x):
    return jax.nn.gelu(x, approximate=True)

def _silu(x):
    return jax.nn.silu(x)

def _sigmoid(x):
    return jax.nn.sigmoid(x)

def _layernorm(x, axis=-1, eps=1e-05):
    m = jnp.mean(x, axis=axis, keepdims=True)
    v = jnp.var(x, axis=axis, keepdims=True)
    return (x - m) / jnp.sqrt(v + eps)

def _scatter_add(tgt, idx, src, axis=0):
    return tgt.at[idx].add(src)

def _segment_sum(src, seg, n):
    return jax.ops.segment_sum(src, seg, n)
kernel_name = 'mk_adj_preln_d2_adj_r2_cf1188'

def setup_inputs(seed: int=0):
    np.random.seed(seed)
    _w = jnp.asarray

    def _rec_inputs():
        import jax
        import jax.numpy as jnp
        _gk = jax.random.key(seed)
        x = 7.22e-05 + 1 * jax.random.normal(jax.random.fold_in(_gk, 1), (2048, 512), jnp.float32)
        _w = (1.0 + jnp.arange(2048, dtype=jnp.float32)) ** (-0.5)
        _w = _w / _w.mean()
        _pij = jnp.clip(0.00195312 * _w[:, None] * _w[None, :], 0.0, 1.0)
        _a = jax.random.uniform(jax.random.fold_in(_gk, 2), (2048, 2048)) < _pij
        _a = jnp.logical_or(_a, jnp.swapaxes(_a, -1, -2))
        _a = jnp.logical_or(_a, jnp.eye(2048, dtype=bool))
        _af = _a.astype(jnp.float32)
        _d = jnp.maximum(_af.sum(-1), 1.0) ** (-0.5)
        _af = _af * _d[..., :, None] * _d[..., None, :]
        adj = _af
        return (x, adj)
    x, adj = _rec_inputs()

    def _L0_gnn_setup():
        import jax, jax.numpy as jnp
        import numpy as np
        N = 4096
        D = 512

        def adjacent_mat(adj):
            adj = adj + jnp.eye(adj.shape[0], dtype=adj.dtype)
            deg = jnp.sum(adj, axis=1)
            dinv = jnp.where(deg > 0, deg ** (-0.5), 0.0).astype(adj.dtype)
            return dinv[:, None] * adj * dinv[None, :]
        key = jax.random.key(seed)
        k1, k2 = jax.random.split(key)
        x = jax.random.normal(k1, (N, D), dtype=jnp.float32)
        Coefficient2 = 1e-08 * jnp.ones((N, N), dtype=jnp.float32)
        A = jax.random.uniform(k2, (N, N), dtype=jnp.float32)
        return {'x': x, 'Coefficient2': Coefficient2, 'A': A}
    _L0_gnn_all = _L0_gnn_setup()
    _L0_gnn_in = {k: v for k, v in _L0_gnn_all.items() if k in ()}
    del _L0_gnn_all

    def _L1_gnn_setup():
        import jax, jax.numpy as jnp
        import numpy as np
        ALPHA = 0.2
        NEG = -9000000000000000.0
        N, NFEAT, NHID, NHEADS = (2048, 512, 64, 8)
        EMB = NHID * NHEADS
        key = jax.random.key(seed)
        ks = jax.random.split(key, 16)
        x = jax.random.normal(ks[0], (N, NFEAT), dtype=jnp.float32)
        adj = (jax.random.uniform(ks[1], (N, N)) < 0.01).astype(jnp.float32)
        adj = jnp.maximum(adj, jnp.eye(N, dtype=jnp.float32))
        s = 0.05
        W = jax.random.normal(ks[2], (NHEADS, NFEAT, NHID), dtype=jnp.float32) * s
        a1 = jax.random.normal(ks[3], (NHEADS, NHID), dtype=jnp.float32) * s
        a2 = jax.random.normal(ks[4], (NHEADS, NHID), dtype=jnp.float32) * s
        W1 = jax.random.normal(ks[5], (EMB // 2, EMB), dtype=jnp.float32) * s
        b1 = jnp.zeros((EMB // 2,), dtype=jnp.float32)
        W2 = jax.random.normal(ks[6], (NFEAT // 4, EMB // 2), dtype=jnp.float32) * s
        b2 = jnp.zeros((NFEAT // 4,), dtype=jnp.float32)
        W3 = jax.random.normal(ks[7], (NFEAT // 2, NFEAT // 4), dtype=jnp.float32) * s
        b3 = jnp.zeros((NFEAT // 2,), dtype=jnp.float32)
        W4 = jax.random.normal(ks[8], (NFEAT, NFEAT // 2), dtype=jnp.float32) * s
        b4 = jnp.zeros((NFEAT,), dtype=jnp.float32)
        return {'x': x, 'adj': adj, 'W': W, 'a1': a1, 'a2': a2, 'W1': W1, 'b1': b1, 'W2': W2, 'b2': b2, 'W3': W3, 'b3': b3, 'W4': W4, 'b4': b4}
    _L1_gnn_all = _L1_gnn_setup()
    _L1_gnn_in = {k: v for k, v in _L1_gnn_all.items() if k in ('W', 'a1', 'a2', 'W1', 'b1', 'W2', 'b2', 'W3', 'b3', 'W4', 'b4')}
    del _L1_gnn_all
    return {'x': x, 'adj': adj, 'L1_gnn_W': _L1_gnn_in['W'], 'L1_gnn_a1': _L1_gnn_in['a1'], 'L1_gnn_a2': _L1_gnn_in['a2'], 'L1_gnn_W1': _L1_gnn_in['W1'], 'L1_gnn_b1': _L1_gnn_in['b1'], 'L1_gnn_W2': _L1_gnn_in['W2'], 'L1_gnn_b2': _L1_gnn_in['b2'], 'L1_gnn_W3': _L1_gnn_in['W3'], 'L1_gnn_b3': _L1_gnn_in['b3'], 'L1_gnn_W4': _L1_gnn_in['W4'], 'L1_gnn_b4': _L1_gnn_in['b4']}

def reference(x, adj, L1_gnn_W, L1_gnn_a1, L1_gnn_a2, L1_gnn_W1, L1_gnn_b1, L1_gnn_W2, L1_gnn_b2, L1_gnn_W3, L1_gnn_b3, L1_gnn_W4, L1_gnn_b4):
    import jax
    import jax.numpy as jnp

    def _L0_gnn_ref(x, Coefficient2, A):
        import jax, jax.numpy as jnp
        import numpy as np
        N = 4096
        D = 512

        def adjacent_mat(adj):
            adj = adj + jnp.eye(adj.shape[0], dtype=adj.dtype)
            deg = jnp.sum(adj, axis=1)
            dinv = jnp.where(deg > 0, deg ** (-0.5), 0.0).astype(adj.dtype)
            return dinv[:, None] * adj * dinv[None, :]
        A_c = jax.lax.stop_gradient(A)
        adj = adjacent_mat((A_c + A_c.T) * 0.5)
        y = Coefficient2 @ adj
        y = y @ x
        return y

    def _L1_gnn_ref(x, adj, W, a1, a2, W1, b1, W2, b2, W3, b3, W4, b4):
        import jax, jax.numpy as jnp
        import numpy as np
        ALPHA = 0.2
        NEG = -9000000000000000.0
        N, NFEAT, NHID, NHEADS = (2048, 512, 64, 8)
        EMB = NHID * NHEADS
        Wh = jnp.einsum('nf,hfd->hnd', x, W)
        e_src = jnp.einsum('hnd,hd->hn', Wh, a1)
        e_dst = jnp.einsum('hnd,hd->hn', Wh, a2)
        e = jax.nn.leaky_relu(e_src[:, :, None] + e_dst[:, None, :], ALPHA)
        e = jnp.where(adj[None] > 0, e, NEG)
        att = jax.nn.softmax(e, axis=-1)
        h = jnp.einsum('hnm,hmd->hnd', att, Wh)
        h = jax.nn.elu(h)
        enc = jnp.transpose(h, (1, 0, 2)).reshape(x.shape[0], -1)
        out = jax.nn.relu(enc @ W1.T + b1)
        out = jax.nn.relu(out @ W2.T + b2)
        out = jax.nn.relu(out @ W3.T + b3)
        out = out @ W4.T + b4
        return out
    h = jnp.maximum(_layernorm(x, axis=-1), 0.0)
    x = x + _L0_gnn_ref(h, adj, adj)
    h = jnp.maximum(_layernorm(x, axis=-1), 0.0)
    x = x + _L1_gnn_ref(h, adj, L1_gnn_W, L1_gnn_a1, L1_gnn_a2, L1_gnn_W1, L1_gnn_b1, L1_gnn_W2, L1_gnn_b2, L1_gnn_W3, L1_gnn_b3, L1_gnn_W4, L1_gnn_b4)
    return x

_drawn_inputs = setup_inputs


def setup_inputs(seed=0):
    import zlib

    import numpy as np

    out = dict(_drawn_inputs(seed))
    spreads = {'L1_gnn_b1': (0.0, 0.73),
     'L1_gnn_b2': (0.0, 0.377),
     'L1_gnn_b3': (0.0, 0.1),
     'L1_gnn_b4': (0.0, 0.1)}
    factors = {'L1_gnn_a1': 8.0, 'L1_gnn_a2': 8.0}
    for name, (base, spread) in spreads.items():
        noise = np.random.default_rng([zlib.crc32(name.encode()), seed]).standard_normal(out[name].shape)
        drawn = base * np.exp(spread * noise) if base else spread * noise
        out[name] = jnp.asarray(drawn.astype(out[name].dtype))
    for name, factor in factors.items():
        out[name] = (out[name] * factor).astype(out[name].dtype)
    return out
```

```python
from contextlib import ExitStack

import concourse.bass as bass
from concourse import mybir

F32 = mybir.dt.float32
F32R = mybir.dt.float32r
U8 = mybir.dt.uint8
ALU = mybir.AluOpType
ACT = mybir.ActivationFunctionType
AX_X = mybir.AxisListType.X

P = 128
N = 2048
F = 512
T = N // P
H = 8
HD = F // H
HE = HD + 1
KC = F // P
G8 = 8
GW = G8 * P
EPS = 1e-5
SLOPE = 0.2
TINY = 1e-30
BANK_TILES = 3
HEAD_BANKS = -(-T // BANK_TILES)


def refine_rsqrt(v, chain, count, d, root, y, tmp):
    v.reciprocal(y, root).then_inc(chain, 1)
    v.wait_ge(chain, count + 1)
    v.tensor_tensor(tmp, y, y, ALU.mult).then_inc(chain, 1)
    v.wait_ge(chain, count + 2)
    v.tensor_tensor(tmp, tmp, d, ALU.mult).then_inc(chain, 1)
    v.wait_ge(chain, count + 3)
    v.tensor_scalar(tmp, tmp, -0.5, 1.5, ALU.mult, ALU.add).then_inc(chain, 1)
    v.wait_ge(chain, count + 4)
    v.tensor_tensor(y, y, tmp, ALU.mult).then_inc(chain, 1)
    v.wait_ge(chain, count + 5)


def split_product(pe, acc, hi, lo, rhs_hi, rhs_lo, first):
    pe.matmul(acc, hi, rhs_hi, start=first, stop=False, skip_group_check=True)
    pe.matmul(acc, hi, rhs_lo, start=False, stop=False, skip_group_check=True)
    return pe.matmul(acc, lo, rhs_hi, start=False, stop=True, skip_group_check=True)


def make_identity(nc, ident):
    with nc.semaphore("ident_zeroed") as zeroed, nc.Block() as block:
        @block.gpsimd
        def _(g):
            g.memset(ident[:], 0.0).then_inc(zeroed, 1)
            g.wait_ge(zeroed, 1)
            g.affine_select(out=ident[:], in_=ident[:], compare_op=ALU.not_equal, fill=1.0, base=0,
                            pattern=[[-1, P]], channel_multiplier=1)


def smooth_features(nc, bank, G, x, adj, adj_t):
    with ExitStack() as ctx:
        def sb(name, shape, dt=F32):
            return ctx.enter_context(nc.sbuf_tensor(name, shape, dt))

        def sem(name):
            return ctx.enter_context(nc.semaphore(name))

        h = sb("l0_h", [P, T, F])
        sum_a = sb("l0_sum_a", [P, 2, GW])
        sum_b = sb("l0_sum_b", [P, T, GW])
        rows_t = sb("l0_rows_t", [P, 2, N])
        s_hi = sb("l0_s_hi", [P, 2, GW], F32R)
        s_lo = sb("l0_s_lo", [P, 2, GW], F32R)
        x_hi = sb("l0_x_hi", [P, 2, F], F32R)
        x_lo = sb("l0_x_lo", [P, 2, F], F32R)
        stats = sb("l0_stats", [P, T, 6])
        mv = sb("l0_mv", [P, T, 2])
        var = sb("l0_var", [P, T])
        root = sb("l0_root", [P, T])
        rstd = sb("l0_rstd", [P, T])
        nmr = sb("l0_nmr", [P, T])
        tmp = sb("l0_tmp", [P, T])
        part = sb("l0_part", [P, 2, 2])
        deg = sb("l0_deg", [P, T, 1])
        degc = sb("l0_degc", [P, T, 1])
        droot = sb("l0_droot", [P, T, 1])
        y = sb("l0_y", [P, T, 1])
        ytmp = sb("l0_ytmp", [P, T, 1])
        dinv = sb("l0_dinv", [P, T, 1])
        hdinv = sb("l0_hdinv", [P, T, 1])

        x_loaded = sem("l0_x_loaded")
        rows_loaded = [sem(f"l0_rows_loaded{b}") for b in range(2)]
        ln_chain = sem("l0_ln_chain")
        var_ready = sem("l0_var_ready")
        ln_root = sem("l0_ln_root")
        norm_ready = sem("l0_norm_ready")
        h_ready = sem("l0_h_ready")
        summed = sem("l0_summed")
        deg_chain = sem("l0_deg_chain")
        deg_ready = sem("l0_deg_ready")
        root_ready = sem("l0_root_ready")
        hi_ready = sem("l0_hi_ready")
        lo_ready = sem("l0_lo_ready")
        x_chain = sem("l0_x_chain")
        x_ready = sem("l0_x_ready")
        slot_free = sem("l0_slot_free")
        acc_done = sem("l0_acc_done")
        base_ready = sem("l0_base_ready")
        g_done = sem("l0_g_done")
        DEG = 9

        with nc.Block() as block:
            @block.sync
            def _(sp):
                sp.dma_start(h[:], x.rearrange("(t p) f -> p t f", p=P)).then_inc(x_loaded, 16)

                def load(i, b):
                    rows = bass.ds(i * P, P)
                    sp.dma_start(rows_t[:, b, :], adj_t[rows, :]).then_inc(rows_loaded[b], 16)
                    sp.dma_start(sum_a[:, b, :], adj[rows, 0:GW]).then_inc(rows_loaded[b], 16)
                    sp.dma_start(sum_b[:, i, :], adj[rows, GW:N]).then_inc(rows_loaded[b], 16)

                load(0, 0)
                load(1, 1)
                with sp.Fori(1, T // 2) as j:
                    for b in range(2):
                        sp.wait_ge(summed, 4 * j + 2 * b - 2)
                        sp.wait_ge(lo_ready, 2 * j + b - 1)
                        load(2 * j + b, b)

            @block.vector
            def _(v):
                v.wait_ge(x_loaded, 16)
                with v.Fori(0, T) as t:
                    v.bn_stats(stats[:, t, :], h[:, t, :]).then_inc(ln_chain, 1)
                v.wait_ge(ln_chain, T)
                for t in range(T):
                    v.bn_aggr(mv[:, t, :], stats[:, t, :]).then_inc(ln_chain, 1)
                v.wait_ge(ln_chain, 2 * T)
                v.tensor_scalar(var[:], mv[:, :, 1], EPS, None, ALU.add).then_inc(var_ready, 1)
                v.wait_ge(ln_root, 1)
                refine_rsqrt(v, ln_chain, 2 * T, var[:], root[:], rstd[:], tmp[:])
                v.scalar_tensor_tensor(out=nmr[:], in0=mv[:, :, 0], scalar=-1.0, in1=rstd[:],
                                       op0=ALU.mult, op1=ALU.mult).then_inc(norm_ready, 1)

                def x_parts(i, b, s):
                    v.wait_ge(slot_free, s + 1)
                    v.tensor_scalar(x_hi[:, b, :], h[:, i, :], dinv[:, i, :], None,
                                    ALU.mult).then_inc(x_chain, 1)
                    v.wait_ge(x_chain, s + 1)
                    v.scalar_tensor_tensor(out=x_lo[:, b, :], in0=h[:, i, :], scalar=dinv[:, i, :],
                                           in1=x_hi[:, b, :].bitcast(F32), op0=ALU.mult,
                                           op1=ALU.subtract).then_inc(x_ready, 1)

                with v.Fori(0, T // 2) as j:
                    for b in range(2):
                        i = 2 * j + b
                        c = DEG * i
                        v.wait_ge(rows_loaded[b], 48 * j + 48)
                        v.scalar_tensor_tensor(out=sum_a[:, b, :], in0=rows_t[:, b, 0:GW], scalar=1.0,
                                               in1=sum_a[:, b, :], op0=ALU.mult, op1=ALU.add,
                                               accum_out=part[:, b, 0:1]).then_inc(summed, 1)
                        v.scalar_tensor_tensor(out=sum_b[:, i, :], in0=rows_t[:, b, GW:N], scalar=1.0,
                                               in1=sum_b[:, i, :], op0=ALU.mult, op1=ALU.add,
                                               accum_out=part[:, b, 1:2]).then_inc(summed, 1)
                        v.wait_ge(summed, 2 * i + 2)
                        v.tensor_tensor(deg[:, i, :], part[:, b, 0:1], part[:, b, 1:2],
                                        ALU.add).then_inc(deg_chain, 1)
                        v.wait_ge(deg_chain, c + 1)
                        v.tensor_scalar(deg[:, i, :], deg[:, i, :], 0.5, 1.0, ALU.mult,
                                        ALU.add).then_inc(deg_chain, 1)
                        v.wait_ge(deg_chain, c + 2)
                        v.tensor_scalar(degc[:, i, :], deg[:, i, :], TINY, None,
                                        ALU.max).then_inc(deg_ready, 1)
                        v.wait_ge(root_ready, i + 1)
                        refine_rsqrt(v, deg_chain, c + 2, degc[:, i, :], droot[:, i, :], y[:, i, :],
                                     ytmp[:, i, :])
                        v.scalar_tensor_tensor(out=dinv[:, i, :], in0=deg[:, i, :], scalar=0.0,
                                               in1=y[:, i, :], op0=ALU.is_gt,
                                               op1=ALU.mult).then_inc(deg_chain, 1)
                        v.wait_ge(deg_chain, c + 8)
                        v.tensor_scalar(hdinv[:, i, :], dinv[:, i, :], 0.5, None,
                                        ALU.mult).then_inc(deg_chain, 1)
                        v.wait_ge(h_ready, i + 1)
                        x_parts(i, b, i)
                v.wait_ge(deg_chain, DEG * T)

                def write_g(g):
                    with v.Fori(0, G8) as k:
                        v.tensor_scalar(G[:, G8 * g + k, :], h[:, G8 * g + k, :], dinv[:, G8 * g + k, :],
                                        dinv[:, G8 * g + k, :], ALU.mult, ALU.mult).then_inc(base_ready, 1)
                    v.wait_ge(base_ready, G8 * (g + 1))
                    for k in range(G8):
                        n = G8 * g + k
                        v.wait_ge(acc_done, n + 1)
                        v.scalar_tensor_tensor(out=G[:, n, :], in0=bank[k][:], scalar=hdinv[:, n, :],
                                               in1=G[:, n, :], op0=ALU.mult, op1=ALU.add).then_inc(g_done, 1)

                write_g(0)
                with v.Fori(0, T // 2) as j:
                    for b in range(2):
                        x_parts(2 * j + b, b, T + 2 * j + b)
                write_g(1)

            @block.scalar
            def _(a):
                a.wait_ge(var_ready, 1)
                a.activation(root[:], var[:], ACT.Sqrt).then_inc(ln_root, 1)
                a.wait_ge(norm_ready, 1)
                with a.Fori(0, T) as t:
                    a.activation(h[:, t, :], h[:, t, :], ACT.Relu, bias=nmr[:, bass.ds(t, 1)],
                                 scale=rstd[:, bass.ds(t, 1)]).then_inc(h_ready, 1)
                with a.Fori(0, T // 2) as j:
                    for b in range(2):
                        i = 2 * j + b
                        a.wait_ge(deg_ready, i + 1)
                        a.activation(droot[:, i, :], degc[:, i, :], ACT.Sqrt).then_inc(root_ready, 1)
                        a.wait_ge(slot_free, i + 1)
                        a.activation(s_hi[:, b, :], sum_a[:, b, :], ACT.Copy).then_inc(hi_ready, 1)
                with a.Fori(0, T // 2) as j:
                    for b in range(2):
                        i = 2 * j + b
                        a.wait_ge(slot_free, T + i + 1)
                        a.activation(s_hi[:, b, :], sum_b[:, i, :], ACT.Copy).then_inc(hi_ready, 1)

            @block.gpsimd
            def _(g):
                with g.Fori(0, T // 2) as j:
                    for b in range(2):
                        g.wait_ge(hi_ready, 2 * j + b + 1)
                        g.tensor_tensor(s_lo[:, b, :], sum_a[:, b, :], s_hi[:, b, :].bitcast(F32),
                                        ALU.subtract).then_inc(lo_ready, 1)
                with g.Fori(0, T // 2) as j:
                    for b in range(2):
                        g.wait_ge(hi_ready, T + 2 * j + b + 1)
                        g.tensor_tensor(s_lo[:, b, :], sum_b[:, 2 * j + b, :], s_hi[:, b, :].bitcast(F32),
                                        ALU.subtract).then_inc(lo_ready, 1)

            @block.tensor
            def _(pe):
                pe.sem_inc(slot_free, 2)

                def products(s, b, g, first, last):
                    pe.wait_ge(lo_ready, s + 1)
                    pe.wait_ge(x_ready, s + 1)
                    for k in range(G8):
                        if first and g == 1:
                            pe.wait_ge(g_done, k + 1)
                        cols = slice(k * P, (k + 1) * P)
                        mm = split_product(pe, bank[k][:], s_hi[:, b, cols], s_lo[:, b, cols],
                                           x_hi[:, b, :], x_lo[:, b, :], first)
                        if last:
                            mm.then_inc(acc_done, 1)
                    if not last:
                        mm.then_inc(slot_free, 1)

                for g in range(2):
                    products(T * g, 0, g, True, False)
                    with pe.Fori(0, T // 2 - 1) as j:
                        products(T * g + 2 * j + 1, 1, g, False, False)
                        products(T * g + 2 * j + 2, 0, g, False, False)
                    products(T * g + T - 1, 1, g, False, True)
                    if g == 0:
                        pe.wait_ge(acc_done, G8)
                        pe.sem_inc(slot_free, 1)


def spread_features(nc, bank, G, x1, mask, rstd, nmr, x, adj_t):
    with ExitStack() as ctx:
        def sb(name, shape, dt=F32):
            return ctx.enter_context(nc.sbuf_tensor(name, shape, dt))

        def sem(name):
            return ctx.enter_context(nc.semaphore(name))

        rows = sb("l1_rows", [P, 4, GW])
        a_hi = sb("l1_a_hi", [P, 2, GW], F32R)
        a_lo = sb("l1_a_lo", [P, 2, GW], F32R)
        g_hi = sb("l1_g_hi", [P, 2, F], F32R)
        g_lo = sb("l1_g_lo", [P, 2, F], F32R)
        stats = sb("l1_stats", [P, T, 6])
        mv = sb("l1_mv", [P, T, 2])
        var = sb("l1_var", [P, T])
        root = sb("l1_root", [P, T])
        tmp = sb("l1_tmp", [P, T])

        x_loaded = sem("l1_x_loaded")
        rows_loaded = [sem(f"l1_rows_loaded{b}") for b in range(4)]
        hi_ready = sem("l1_hi_ready")
        lo_ready = sem("l1_lo_ready")
        g_chain = sem("l1_g_chain")
        g_ready = sem("l1_g_ready")
        mask_done = sem("l1_mask_done")
        slot_free = sem("l1_slot_free")
        acc_done = sem("l1_acc_done")
        x1_done = sem("l1_x1_done")
        ln_chain = sem("l1_ln_chain")
        var_ready = sem("l1_var_ready")
        ln_root = sem("l1_ln_root")

        with nc.Block() as block:
            @block.sync
            def _(sp):
                def load(g, i, r):
                    sp.dma_start(rows[:, r, :], adj_t[bass.ds(i * P, P), g * GW:(g + 1) * GW]
                                 ).then_inc(rows_loaded[r], 16)

                for r in range(4):
                    load(0, r, r)
                sp.dma_start(x1[:], x.rearrange("(t p) f -> p t f", p=P)).then_inc(x_loaded, 16)
                for g in range(2):
                    with sp.Fori(1 - g, T // 4) as j:
                        for r in range(4):
                            sp.wait_ge(lo_ready, T * g + 4 * j + r - 3)
                            sp.wait_ge(mask_done, T * g + 4 * j + r - 3)
                            load(g, 4 * j + r, r)

            def steps(eng, body):
                for g in range(2):
                    with eng.Fori(0, T // 4) as j:
                        for r in range(4):
                            body(g, 4 * j + r, r, T * g + 4 * j + r, 4 * g + j)

            @block.scalar
            def _(a):
                def cut_hi(g, i, r, s, turn):
                    a.wait_ge(rows_loaded[r], 16 * turn + 16)
                    a.wait_ge(slot_free, s + 1)
                    a.activation(a_hi[:, r % 2, :], rows[:, r, :], ACT.Copy).then_inc(hi_ready, 1)
                steps(a, cut_hi)
                a.wait_ge(var_ready, 1)
                a.activation(root[:], var[:], ACT.Sqrt).then_inc(ln_root, 1)

            @block.vector
            def _(v):
                def cut(g, i, r, s, turn):
                    b = r % 2
                    v.wait_ge(slot_free, s + 1)
                    v.tensor_copy(g_hi[:, b, :], G[:, i, :]).then_inc(g_chain, 1)
                    v.wait_ge(g_chain, s + 1)
                    v.tensor_tensor(g_lo[:, b, :], G[:, i, :], g_hi[:, b, :].bitcast(F32),
                                    ALU.subtract).then_inc(g_ready, 1)
                    v.wait_ge(hi_ready, s + 1)
                    v.tensor_tensor(a_lo[:, b, :], rows[:, r, :], a_hi[:, b, :].bitcast(F32),
                                    ALU.subtract).then_inc(lo_ready, 1)
                    v.tensor_scalar(mask[:, i, g * GW:(g + 1) * GW], rows[:, r, :], 0.0, None,
                                    ALU.is_gt).then_inc(mask_done, 1)

                def add_y(g):
                    for k in range(G8):
                        n = G8 * g + k
                        v.wait_ge(acc_done, n + 1)
                        v.tensor_tensor(x1[:, n, :], bank[k][:], x1[:, n, :], ALU.add).then_inc(x1_done, 1)

                def stats_of(g):
                    v.wait_ge(x1_done, G8 * (g + 1))
                    with v.Fori(0, G8) as k:
                        v.bn_stats(stats[:, G8 * g + k, :], x1[:, G8 * g + k, :]).then_inc(ln_chain, 1)

                with v.Fori(0, T // 4) as j:
                    for r in range(4):
                        cut(0, 4 * j + r, r, 4 * j + r, j)
                v.wait_ge(x_loaded, 16)
                add_y(0)
                with v.Fori(0, T // 4) as j:
                    for r in range(4):
                        cut(1, 4 * j + r, r, T + 4 * j + r, 4 + j)
                stats_of(0)
                add_y(1)
                stats_of(1)
                v.wait_ge(ln_chain, T)
                for t in range(T):
                    v.bn_aggr(mv[:, t, :], stats[:, t, :]).then_inc(ln_chain, 1)
                v.wait_ge(ln_chain, 2 * T)
                v.tensor_scalar(var[:], mv[:, :, 1], EPS, None, ALU.add).then_inc(var_ready, 1)
                v.wait_ge(ln_root, 1)
                refine_rsqrt(v, ln_chain, 2 * T, var[:], root[:], rstd[:], tmp[:])
                v.scalar_tensor_tensor(out=nmr[:], in0=mv[:, :, 0], scalar=-1.0, in1=rstd[:],
                                       op0=ALU.mult, op1=ALU.mult)

            @block.tensor
            def _(pe):
                pe.sem_inc(slot_free, 2)

                def products(s, b, g, first, last):
                    pe.wait_ge(g_ready, s + 1)
                    pe.wait_ge(lo_ready, s + 1)
                    for k in range(G8):
                        if first and g == 1:
                            pe.wait_ge(x1_done, k + 1)
                        cols = slice(k * P, (k + 1) * P)
                        mm = split_product(pe, bank[k][:], a_hi[:, b, cols], a_lo[:, b, cols],
                                           g_hi[:, b, :], g_lo[:, b, :], first)
                        if last:
                            mm.then_inc(acc_done, 1)
                    if not last:
                        mm.then_inc(slot_free, 1)

                for g in range(2):
                    products(T * g, 0, g, True, False)
                    with pe.Fori(0, T // 2 - 1) as j:
                        products(T * g + 2 * j + 1, 1, g, False, False)
                        products(T * g + 2 * j + 2, 0, g, False, False)
                    products(T * g + T - 1, 1, g, False, True)
                    if g == 0:
                        pe.wait_ge(acc_done, G8)
                        pe.sem_inc(slot_free, 1)


def project_heads(nc, bank, x1, rstd, nmr, wh, e, ident, w, a1, a2, src_rows, dst_range, x1_store):
    with ExitStack() as ctx:
        def sb(name, shape, dt=F32):
            return ctx.enter_context(nc.sbuf_tensor(name, shape, dt))

        def sem(name):
            return ctx.enter_context(nc.semaphore(name))

        w_f = sb("l2_w", [P, KC, H, HD])
        w_hi = sb("l2_w_hi", [P, KC, F], F32R)
        w_lo = sb("l2_w_lo", [P, KC, F], F32R)
        a_b = sb("l2_a", [P, 2, F])
        h2 = sb("l2_h", [P, 2, F])
        ht_hi = sb("l2_ht_hi", [P, 2, F], F32R)
        ht_lo = sb("l2_ht_lo", [P, 2, F], F32R)
        prod = sb("l2_prod", [P, 2, 2, F])
        e_t = sb("l2_e_t", [2 * H, N])
        top = sb("l2_top", [2 * H, 1])

        loaded = sem("l2_loaded")
        w_chain = sem("l2_w_chain")
        w_ready = sem("l2_w_ready")
        ones_ready = sem("l2_ones_ready")
        h_ready = sem("l2_h_ready")
        turned = sem("l2_turned")
        hi_ready = sem("l2_hi_ready")
        lo_ready = sem("l2_lo_ready")
        acc_done = sem("l2_acc_done")
        wh_ready = sem("l2_wh_ready")
        prod_ready = sem("l2_prod_ready")
        e_ready = sem("l2_e_ready")
        e_turned = sem("l2_e_turned")
        e_copied = sem("l2_e_copied")
        top_ready = sem("l2_top_ready")
        stored = sem("l2_stored")
        top_stored = sem("l2_top_stored")
        x1_stored = sem("l2_x1_stored")

        with nc.Block() as block:
            @block.sync
            def _(sp):
                sp.dma_start(x1_store.rearrange("(t p) f -> p t f", p=P), x1[:]).then_inc(x1_stored, 16)
                for k in range(KC):
                    sp.dma_start(w_f[:, k, :, :], w[:, k * P:(k + 1) * P, :].rearrange("h p d -> p h d")
                                 ).then_inc(loaded, 16)
                for n, a in enumerate((a1, a2)):
                    row = a.rearrange("h d -> (h d)").rearrange("(o f) -> o f", o=1)
                    sp.dma_start(a_b[:, n, :], row.to_broadcast([P, F])).then_inc(loaded, 16)
                sp.wait_ge(e_copied, 4)
                sp.dma_start(src_rows, e_t[0:H, :]).then_inc(stored, 16)
                sp.wait_ge(top_ready, 1)
                sp.dma_start(dst_range, top[H:2 * H, :]).then_inc(top_stored, 16)
                sp.wait_ge(stored, 16)
                sp.wait_ge(top_stored, 16)
                sp.wait_ge(x1_stored, 16)

            @block.scalar
            def _(a):
                def normalise(t, b):
                    a.wait_ge(turned, t + 1)
                    a.activation(h2[:, b, :], x1[:, t, :], ACT.Relu, bias=nmr[:, bass.ds(t, 1)],
                                 scale=rstd[:, bass.ds(t, 1)]).then_inc(h_ready, 1)

                def tile(t, b, last):
                    a.wait_ge(turned, t + 3)
                    a.wait_ge(acc_done, t + 1)
                    a.activation(ht_hi[:, b, :], bank[b][:], ACT.Copy).then_inc(hi_ready, 1)
                    if not last:
                        normalise(t + 1, 1 - b)
                    a.wait_ge(acc_done, t + 3)
                    a.activation(wh[:, t, :, 0:HD], bank[2 + b][:].rearrange("p (h d) -> p h d", h=H),
                                 ACT.Copy).then_inc(wh_ready, 1)

                a.sem_inc(wh_ready, 2)
                normalise(0, 0)
                with a.Fori(0, T // 2 - 1) as j:
                    for b in range(2):
                        tile(2 * j + b, b, False)
                tile(T - 2, 0, False)
                tile(T - 1, 1, True)

            @block.vector
            def _(v):
                v.memset(wh[:, :, :, HD:HE], 1.0).then_inc(ones_ready, 1)
                v.wait_ge(loaded, 16 * (KC + 2))
                v.tensor_copy(w_hi[:], w_f[:].rearrange("p k h d -> p k (h d)")).then_inc(w_chain, 1)
                v.wait_ge(w_chain, 1)
                v.tensor_tensor(w_lo[:], w_f[:].rearrange("p k h d -> p k (h d)"), w_hi[:].bitcast(F32),
                                ALU.subtract).then_inc(w_ready, 1)
                v.sem_inc(e_ready, 4)
                with v.Fori(0, T // 2) as j:
                    for b in range(2):
                        t = 2 * j + b
                        v.wait_ge(hi_ready, t + 1)
                        v.tensor_tensor(ht_lo[:, b, :], bank[b][:], ht_hi[:, b, :].bitcast(F32),
                                        ALU.subtract).then_inc(lo_ready, 1)
                        v.wait_ge(wh_ready, t + 3)
                        v.wait_ge(e_ready, 2 * t + 2)
                        for n in range(2):
                            v.tensor_tensor(prod[:, b, n, :].rearrange("p (h d) -> p h d", h=H),
                                            wh[:, t, :, 0:HD],
                                            a_b[:, n, :].rearrange("p (h d) -> p h d", h=H),
                                            ALU.mult).then_inc(prod_ready, 1)
                        for n in range(2):
                            v.wait_ge(prod_ready, 2 * t + n + 1)
                            v.tensor_reduce(e[:, t, n * H:(n + 1) * H],
                                            prod[:, b, n, :].rearrange("p (h d) -> p h d", h=H),
                                            AX_X, ALU.add).then_inc(e_ready, 1)
                for q in range(4):
                    v.wait_ge(e_turned, q + 1)
                    v.tensor_copy(e_t[:, q * 512:(q + 1) * 512], bank[4 + q][0:2 * H, :]).then_inc(e_copied, 1)
                v.wait_ge(e_copied, 4)
                v.tensor_reduce(top[:], e_t[:], AX_X, ALU.max).then_inc(top_ready, 1)

            @block.tensor
            def _(pe):
                pe.sem_inc(turned, 2)
                pe.sem_inc(acc_done, 2)
                pe.wait_ge(w_ready, 1)

                def turn(t, b):
                    pe.wait_ge(h_ready, t + 1)
                    for k in range(KC):
                        cols = slice(k * P, (k + 1) * P)
                        mm = pe.transpose(bank[b][:, cols], h2[:, b, cols], ident[:])
                    mm.then_inc(turned, 1)

                def tile(t, b, last):
                    if not last:
                        turn(t + 1, 1 - b)
                    pe.wait_ge(lo_ready, t + 1)
                    pe.wait_ge(wh_ready, t + 1)
                    for k in range(KC):
                        cols = slice(k * P, (k + 1) * P)
                        mm = split_product(pe, bank[2 + b][:], ht_hi[:, b, cols], ht_lo[:, b, cols],
                                           w_hi[:, k, :], w_lo[:, k, :], k == 0)
                    mm.then_inc(acc_done, 1)

                turn(0, 0)
                with pe.Fori(0, T // 2 - 1) as j:
                    for b in range(2):
                        tile(2 * j + b, b, False)
                tile(T - 2, 0, False)
                tile(T - 1, 1, True)
                pe.wait_ge(e_ready, 2 * T + 4)
                for t in range(T):
                    mm = pe.transpose(bank[4 + t // 4][0:2 * H, (t % 4) * P:(t % 4 + 1) * P], e[:, t, :], ident[:])
                    if t % 4 == 3:
                        mm.then_inc(e_turned, 1)


def edge_factors(nc, bank, wh, e, mask, fac, neg_d, md, dst_range):
    with ExitStack() as ctx:
        def sb(name, shape, dt=F32):
            return ctx.enter_context(nc.sbuf_tensor(name, shape, dt))

        def sem(name):
            return ctx.enter_context(nc.semaphore(name))

        top = sb("l3_top", [P, 1, H])
        t1 = sb("l3_t1", [P, T, H])
        t2 = sb("l3_t2", [P, T, H])
        t3 = sb("l3_t3", [P, T, H])
        c_hi = sb("l3_c_hi", [P, T, H], F32R)
        c_lo = sb("l3_c_lo", [P, T, H], F32R)
        cw = sb("l3_cw", [P, 2, F])
        cw_hi = sb("l3_cw_hi", [P, 2, F], F32R)
        cw_lo = sb("l3_cw_lo", [P, 2, F], F32R)
        m_r = sb("l3_mask_r", [P, 2, 6 * P], F32R)
        GROUPS = ((0, 6), (6, 5), (11, 5))

        loaded = sem("l3_loaded")
        chain = sem("l3_chain")
        args_ready = sem("l3_args_ready")
        fac_ready = sem("l3_fac_ready")
        c_chain = sem("l3_c_chain")
        c_ready = sem("l3_c_ready")
        cw_ready = sem("l3_cw_ready")
        cw_hi_ready = sem("l3_cw_hi_ready")
        cw_lo_ready = sem("l3_cw_lo_ready")
        mask_ready = sem("l3_mask_ready")
        slot_free = sem("l3_slot_free")
        acc_done = sem("l3_acc_done")
        md_done = sem("l3_md_done")

        def bcast_t(ap):
            return ap.to_broadcast([P, T, H])

        with nc.Block() as block:
            @block.sync
            def _(sp):
                sp.dma_start(top[:, 0, :], dst_range.rearrange("h o -> o h").to_broadcast([P, H])
                             ).then_inc(loaded, 16)

            @block.vector
            def _(v):
                v.wait_ge(loaded, 16)
                src, dst = e[:, :, 0:H], e[:, :, H:2 * H]
                v.tensor_tensor(t1[:], dst, bcast_t(top[:]), ALU.subtract).then_inc(args_ready, 1)
                v.tensor_tensor(t2[:], src, bcast_t(top[:]), ALU.add).then_inc(chain, 1)
                v.tensor_scalar(neg_d[:], dst, -1.0, None, ALU.mult).then_inc(chain, 1)
                v.wait_ge(chain, 2)
                v.tensor_scalar(t3[:], t2[:], 1.0 - SLOPE, 0.0, ALU.mult, ALU.min).then_inc(args_ready, 1)
                v.wait_ge(args_ready, 2)
                v.tensor_scalar(t2[:], t2[:], SLOPE - 1.0, 0.0, ALU.mult, ALU.min).then_inc(args_ready, 1)
                v.wait_ge(fac_ready, 4)
                v.tensor_copy(c_hi[:], fac["C"][:]).then_inc(c_chain, 1)
                v.wait_ge(c_chain, 1)
                v.tensor_tensor(c_lo[:], fac["C"][:], c_hi[:].bitcast(F32), ALU.subtract).then_inc(c_ready, 1)
                for g, (n0, cnt) in enumerate(GROUPS):
                    with v.Fori(0, T // 2) as j:
                        for b in range(2):
                            i = 2 * j + b
                            s = T * g + i
                            v.wait_ge(slot_free, s + 1)
                            v.tensor_tensor(cw[:, b, :].rearrange("p (h d) -> p h d", h=H), wh[:, i, :, 0:HD],
                                            fac["C"][:, i, :].unsqueeze(2).to_broadcast([P, H, HD]),
                                            ALU.mult).then_inc(cw_ready, 1)
                            v.wait_ge(cw_hi_ready, s + 1)
                            v.tensor_tensor(cw_lo[:, b, :], cw[:, b, :], cw_hi[:, b, :].bitcast(F32),
                                            ALU.subtract).then_inc(cw_lo_ready, 1)
                    for k in range(cnt):
                        n = n0 + k
                        v.wait_ge(acc_done, n + 1)
                        d = fac["D"][:, n, :].unsqueeze(2)
                        v.tensor_tensor(md[:, n, :, 0:HD], bank[k][:].rearrange("p (h d) -> p h d", h=H),
                                        d.to_broadcast([P, H, HD]), ALU.mult).then_inc(md_done, 1)
                        if k == cnt - 1:
                            v.tensor_tensor(md[:, n0:n0 + cnt, :, HD],
                                            bank[7][:, 0:cnt * H].rearrange("p (k h) -> p k h", h=H),
                                            fac["D"][:, n0:n0 + cnt, :], ALU.mult).then_inc(md_done, 1)

            @block.scalar
            def _(a):
                a.wait_ge(args_ready, 1)
                a.activation(fac["A"][:], t1[:], ACT.Exp).then_inc(fac_ready, 1)
                a.activation(fac["C"][:], t1[:], ACT.Exp, scale=SLOPE).then_inc(fac_ready, 1)
                a.wait_ge(args_ready, 3)
                a.activation(fac["B"][:], t3[:], ACT.Exp).then_inc(fac_ready, 1)
                a.activation(fac["D"][:], t2[:], ACT.Exp).then_inc(fac_ready, 1)
                for g, (n0, cnt) in enumerate(GROUPS):
                    with a.Fori(0, T // 2) as j:
                        for b in range(2):
                            i = 2 * j + b
                            s = T * g + i
                            a.wait_ge(slot_free, s + 1)
                            a.activation(m_r[:, b, 0:cnt * P], mask[:, i, n0 * P:(n0 + cnt) * P],
                                         ACT.Copy).then_inc(mask_ready, 1)
                            a.wait_ge(cw_ready, s + 1)
                            a.activation(cw_hi[:, b, :], cw[:, b, :], ACT.Copy).then_inc(cw_hi_ready, 1)

            @block.tensor
            def _(pe):
                pe.sem_inc(slot_free, 2)
                pe.wait_ge(c_ready, 1)

                def products(s, i, b, g, first, last):
                    n0, cnt = GROUPS[g]
                    pe.wait_ge(mask_ready, s + 1)
                    pe.wait_ge(cw_lo_ready, s + 1)
                    if first and g:
                        pe.wait_ge(md_done, n0 + g)
                    for k in range(cnt):
                        blk = m_r[:, b, k * P:(k + 1) * P]
                        den = bank[7][:, k * H:(k + 1) * H]
                        pe.matmul(bank[k][:], blk, cw_hi[:, b, :], start=first, stop=False, skip_group_check=True)
                        pe.matmul(bank[k][:], blk, cw_lo[:, b, :], start=False, stop=True, skip_group_check=True)
                        pe.matmul(den, blk, c_hi[:, i, :], start=first and k == 0, stop=False,
                                  skip_group_check=True)
                        mm = pe.matmul(den, blk, c_lo[:, i, :], start=False, stop=True, skip_group_check=True)
                        if last:
                            mm.then_inc(acc_done, 1)
                    if not last:
                        mm.then_inc(slot_free, 1)

                for g in range(len(GROUPS)):
                    products(T * g, 0, 0, g, True, False)
                    with pe.Fori(0, T // 2 - 1) as j:
                        products(T * g + 2 * j + 1, 2 * j + 1, 1, g, False, False)
                        products(T * g + 2 * j + 2, 2 * j + 2, 0, g, False, False)
                    products(T * g + T - 1, T - 1, 1, g, False, True)
                    if g < len(GROUPS) - 1:
                        pe.wait_ge(acc_done, sum(GROUPS[g]))
                        pe.sem_inc(slot_free, 1)


def attend(nc, bank, wh, mask, fac, neg_d, md, src_rows):
    with ExitStack() as ctx:
        def sb(name, shape, dt=F32):
            return ctx.enter_context(nc.sbuf_tensor(name, shape, dt))

        def sem(name):
            return ctx.enter_context(nc.semaphore(name))

        PW = 2 * HE
        QR = 4
        src = sb("l4_src", [P, 2, N])
        q = sb("l4_q", [P, QR, N], F32R)
        whole = sb("l4_whole", [P, T, PW])
        parts = sb("l4_parts", [P, 2, T, 2, PW], F32R)
        o = sb("l4_o", [P, T, PW])
        rden = sb("l4_rden", [P, T, 1])

        src_loaded = [sem(f"l4_src_loaded{b}") for b in range(2)]
        whole_ready = sem("l4_whole_ready")
        part_hi = sem("l4_part_hi")
        part_lo = sem("l4_part_lo")
        q_ready = sem("l4_q_ready")
        acc_done = sem("l4_acc_done")
        acc_free = sem("l4_acc_free")
        scaled = sem("l4_scaled")
        o_free = sem("l4_o_free")
        rden_ready = sem("l4_rden_ready")
        EARLY = QR * HEAD_BANKS

        def heads(eng, body):
            body(0, 0, 0, True, False)
            with eng.Fori(0, H // 2 - 1) as j:
                body(2 * j + 1, 1, j, False, False)
                body(2 * j + 2, 0, j + 1, False, False)
            body(H - 1, 1, H // 2 - 1, False, True)

        def of_head(ap, h, cols=slice(0, HE)):
            return ap[:, :, bass.ds(h, 1), cols].rearrange("p t o e -> p t (o e)")

        with nc.Block() as block:
            @block.sync
            def _(sp):
                def load(h, b):
                    sp.dma_start(src[:, b, :], src_rows[bass.ds(h, 1), :].to_broadcast([P, N])
                                 ).then_inc(src_loaded[b], 16)
                load(0, 0)
                load(1, 1)
                with sp.Fori(1, H // 2) as hp:
                    for hb in range(2):
                        sp.wait_ge(q_ready, 2 * T * hp + T * (hb - 1))
                        load(2 * hp + hb, hb)

            @block.vector
            def _(v):
                def scale_wh(h):
                    for n, f in enumerate(("A", "C")):
                        v.tensor_tensor(whole[:, :, n * HE:(n + 1) * HE], of_head(wh, h),
                                        fac[f][:, :, bass.ds(h, 1)].to_broadcast([P, T, HE]),
                                        ALU.mult).then_inc(whole_ready, 1)

                def choose(h, slot, i0, i1):
                    for i in range(i0, i1):
                        v.wait_ge(acc_done, HEAD_BANKS * (T * h + i + 1))
                        v.scalar_tensor_tensor(out=q[:, i % QR, :], in0=src[:, slot, :],
                                               scalar=neg_d[:, i, bass.ds(h, 1)], in1=mask[:, i, :],
                                               op0=ALU.is_ge, op1=ALU.mult).then_inc(q_ready, 1)

                def invert(h):
                    v.wait_ge(scaled, 4 * h + 4)
                    v.wait_ge(o_free, h + 1)
                    v.reciprocal(rden[:], o[:, :, HD:HE]).then_inc(rden_ready, 1)

                def head(h, slot, turn, first, last):
                    if not last:
                        v.wait_ge(part_lo, 2 * h + 2)
                        scale_wh(h + 1)
                    v.wait_ge(src_loaded[slot], 16 * turn + 16)
                    choose(h, slot, 0, T - 4)
                    if not first:
                        invert(h - 1)
                    choose(h, slot, T - 4, T)

                scale_wh(0)
                heads(v, head)
                invert(H - 1)

            @block.scalar
            def _(a):
                a.sem_inc(acc_free, HEAD_BANKS)

                def cut_hi(h, slot):
                    for n in range(2):
                        cols = slice(n * HE, (n + 1) * HE)
                        a.wait_ge(whole_ready, 2 * h + n + 1)
                        a.activation(parts[:, slot, :, 0, cols], whole[:, :, cols], ACT.Copy).then_inc(part_hi, 1)

                def head(h, slot, turn, first, last):
                    if not last:
                        cut_hi(h + 1, 1 - slot)
                    a.wait_ge(o_free, h + 1)
                    for k in range(HEAD_BANKS):
                        t0 = BANK_TILES * k
                        cnt = min(BANK_TILES, T - t0)
                        a.wait_ge(acc_done, EARLY + HEAD_BANKS * (T * h + T - 1) + k + 1)
                        a.activation(o[:, t0:t0 + cnt, :],
                                     bank[k][:, 0:cnt * PW].rearrange("p (t c) -> p t c", c=PW),
                                     ACT.Copy).then_inc(acc_free, 1)

                cut_hi(0, 0)
                heads(a, head)

            @block.gpsimd
            def _(p):
                p.sem_inc(o_free, 1)

                def cut_lo(h, slot):
                    for n in range(2):
                        cols = slice(n * HE, (n + 1) * HE)
                        p.wait_ge(part_hi, 2 * h + n + 1)
                        p.tensor_tensor(parts[:, slot, :, 1, cols], whole[:, :, cols],
                                        parts[:, slot, :, 0, cols].bitcast(F32),
                                        ALU.subtract).then_inc(part_lo, 1)

                def head(h, slot, turn, first, last):
                    if not last:
                        cut_lo(h + 1, 1 - slot)
                    p.wait_ge(acc_free, HEAD_BANKS * (h + 2))
                    for n, f in enumerate(("B", "D")):
                        cols = slice(n * HE, (n + 1) * HE)
                        p.tensor_tensor(o[:, :, cols], o[:, :, cols],
                                        fac[f][:, :, bass.ds(h, 1)].to_broadcast([P, T, HE]),
                                        ALU.mult).then_inc(scaled, 1)
                    p.wait_ge(scaled, 4 * h + 2)
                    p.tensor_tensor(o[:, :, 0:HE], o[:, :, 0:HE], o[:, :, HE:PW], ALU.subtract
                                    ).then_inc(scaled, 1)
                    p.wait_ge(scaled, 4 * h + 3)
                    p.tensor_tensor(o[:, :, 0:HE], o[:, :, 0:HE], of_head(md, h), ALU.add
                                    ).then_inc(scaled, 1)
                    p.wait_ge(rden_ready, h + 1)
                    p.tensor_tensor(of_head(wh, h, slice(0, HD)), o[:, :, 0:HD],
                                    rden[:].to_broadcast([P, T, HD]), ALU.mult).then_inc(o_free, 1)

                cut_lo(0, 0)
                heads(p, head)

            @block.tensor
            def _(pe):
                pe.sem_inc(acc_done, EARLY)

                def products(h, i, b, slot, first):
                    pe.wait_ge(q_ready, T * h + i + 1)
                    for t in range(T):
                        k, c = divmod(t, BANK_TILES)
                        if first and c == 0:
                            pe.wait_ge(acc_free, HEAD_BANKS * h + k + 1)
                        acc = bank[k][:, c * PW:(c + 1) * PW]
                        blk = q[:, b, t * P:(t + 1) * P]
                        pe.matmul(acc, blk, parts[:, slot, i, 0, :], start=first and c == 0, stop=False,
                                  skip_group_check=True)
                        mm = pe.matmul(acc, blk, parts[:, slot, i, 1, :], start=False, stop=True,
                                       skip_group_check=True)
                        if c == BANK_TILES - 1 or t == T - 1:
                            mm.then_inc(acc_done, 1)

                with pe.Fori(0, H // 2) as hp:
                    for slot in range(2):
                        h = 2 * hp + slot
                        pe.wait_ge(part_lo, 2 * h + 2)
                        for b in range(QR):
                            products(h, b, b, slot, b == 0)
                        with pe.Fori(1, T // QR) as j:
                            for b in range(QR):
                                products(h, QR * j + b, b, slot, False)


def feed_forward(nc, bank, wh, ident, x1_store, w1_t, b1, w2_t, b2, w3_t, b3, w4_t, b4, out):
    F1, F2, F3 = w1_t.shape[1], w2_t.shape[1], w3_t.shape[1]
    K1, K3 = F1 // P, F3 // P
    TC = 4
    CW = TC * P
    with ExitStack() as ctx:
        def sb(name, shape, dt=F32):
            return ctx.enter_context(nc.sbuf_tensor(name, shape, dt))

        def sem(name):
            return ctx.enter_context(nc.semaphore(name))

        w1_s = sb("l5_w1", [P, KC, F1])
        w2_s = sb("l5_w2", [P, K1, F2])
        w3_s = sb("l5_w3", [P, F3])
        w4_s = sb("l5_w4", [P, K3, F])
        b1_s = sb("l5_b1", [P, K1])
        b2_s = sb("l5_b2", [P, 1])
        b3_s = sb("l5_b3", [P, K3])
        b4_s = sb("l5_b4", [P, 1, F])
        neg = sb("l5_neg", [P, TC * H, HD])
        enc = sb("l5_enc", [P, TC, F])
        enc_t = sb("l5_enc_t", [P, KC, CW])
        o1 = sb("l5_o1", [P, K1, CW])
        o2 = sb("l5_o2", [P, CW])
        o3 = sb("l5_o3", [P, K3, CW])
        res = sb("l5_res", [P, TC, F])

        w_loaded = sem("l5_w_loaded")
        x_loaded = sem("l5_x_loaded")
        neg_ready = sem("l5_neg_ready")
        exp_ready = sem("l5_exp_ready")
        pos_ready = sem("l5_pos_ready")
        enc_ready = sem("l5_enc_ready")
        turned = sem("l5_turned")
        enc_t_ready = sem("l5_enc_t_ready")
        sums_done = sem("l5_sums_done")
        act_ready = sem("l5_act_ready")
        biased = sem("l5_biased")
        rows_done = sem("l5_rows_done")
        out_ready = sem("l5_out_ready")
        stored = sem("l5_stored")
        zs = wh[:].rearrange("p t h e -> p (t h) e")

        with nc.Block() as block:
            @block.sync
            def _(sp):
                for dst, src in ((w1_s, w1_t.rearrange("(k p) f -> p k f", p=P)),
                                 (w2_s, w2_t.rearrange("(k p) f -> p k f", p=P)),
                                 (w3_s, w3_t), (w4_s, w4_t.rearrange("(k p) f -> p k f", p=P)),
                                 (b1_s, b1), (b2_s, b2), (b3_s, b3)):
                    sp.dma_start(dst[:], src).then_inc(w_loaded, 16)
                sp.dma_start(b4_s[:, 0, :], b4.rearrange("(o f) -> o f", o=1).to_broadcast([P, F])
                             ).then_inc(w_loaded, 16)
                sp.sem_inc(stored, 16)
                with sp.Fori(0, T // TC) as c:
                    rows = bass.ds(c * CW, CW)
                    sp.wait_ge(stored, 16 * c + 16)
                    sp.dma_start(res[:], x1_store[rows, :].rearrange("(t p) f -> p t f", p=P)
                                 ).then_inc(x_loaded, 16)
                    sp.wait_ge(out_ready, TC * c + 2 * TC)
                    sp.dma_start(out[rows, :].rearrange("(t p) f -> p t f", p=P), res[:]).then_inc(stored, 16)
                sp.wait_ge(stored, 16 * (T // TC + 1))

            @block.vector
            def _(v):
                v.sem_inc(enc_ready, 1)
                v.sem_inc(out_ready, TC)
                v.wait_ge(w_loaded, 16 * 8)
                with v.Fori(0, T // TC) as c:
                    z = zs[:, bass.ds(c * TC * H, TC * H), 0:HD]
                    v.wait_ge(enc_ready, c + 1)
                    v.tensor_scalar(neg[:], z, 0.0, None, ALU.min).then_inc(neg_ready, 1)
                    v.wait_ge(turned, KC * c + KC)
                    enc_z = enc[:].rearrange("p t (h d) -> p (t h) d", h=H)
                    v.tensor_scalar(enc_z, z, 0.0, -1.0, ALU.max, ALU.add).then_inc(pos_ready, 1)
                    v.wait_ge(exp_ready, c + 1)
                    v.wait_ge(pos_ready, c + 1)
                    v.tensor_tensor(enc_z, enc_z, neg[:], ALU.add).then_inc(enc_ready, 1)
                    for k in range(KC):
                        v.wait_ge(turned, KC * c + KC + k + 1)
                        v.tensor_copy(enc_t[:, k, :], bank[k][:]).then_inc(enc_t_ready, 1)
                    v.wait_ge(x_loaded, 16 * c + 16)
                    v.tensor_tensor(res[:], res[:], b4_s[:].to_broadcast([P, TC, F]), ALU.add).then_inc(biased, 1)
                    v.wait_ge(biased, c + 1)
                    for t in range(TC):
                        v.wait_ge(rows_done, TC * c + t + 1)
                        v.tensor_tensor(res[:, t, :], bank[t][:], res[:, t, :], ALU.add).then_inc(out_ready, 1)

            @block.scalar
            def _(a):
                a.wait_ge(w_loaded, 16 * 8)
                with a.Fori(0, T // TC) as c:
                    a.wait_ge(neg_ready, c + 1)
                    a.activation(neg[:], neg[:], ACT.Exp).then_inc(exp_ready, 1)
                    a.wait_ge(sums_done, 5 * c + 2)
                    for k in range(K1):
                        a.activation(o1[:, k, :], bank[4 + k][:], ACT.Relu, bias=b1_s[:, k:k + 1]
                                     ).then_inc(act_ready, 1)
                    a.wait_ge(sums_done, 5 * c + 3)
                    a.activation(o2[:], bank[6][:], ACT.Relu, bias=b2_s[:, 0:1]).then_inc(act_ready, 1)
                    a.wait_ge(sums_done, 5 * c + 5)
                    for k in range(K3):
                        a.activation(o3[:, k, :], bank[4 + k][:], ACT.Relu, bias=b3_s[:, k:k + 1]
                                     ).then_inc(act_ready, 1)

            @block.tensor
            def _(pe):
                pe.sem_inc(turned, KC)
                pe.wait_ge(w_loaded, 16 * 8)
                with pe.Fori(0, T // TC) as c:
                    pe.wait_ge(enc_ready, c + 2)
                    for k in range(KC):
                        pe.wait_ge(out_ready, TC * c + k + 1)
                        for t in range(TC):
                            mm = pe.transpose(bank[k][:, t * P:(t + 1) * P], enc[:, t, k * P:(k + 1) * P], ident[:])
                        mm.then_inc(turned, 1)
                    pe.wait_ge(enc_t_ready, KC * c + KC)
                    for m in range(K1):
                        for k in range(KC):
                            mm = pe.matmul(bank[4 + m][:], w1_s[:, k, m * P:(m + 1) * P], enc_t[:, k, :],
                                           start=k == 0, stop=k == KC - 1)
                        mm.then_inc(sums_done, 1)
                    pe.wait_ge(act_ready, 5 * c + 2)
                    for k in range(K1):
                        mm = pe.matmul(bank[6][:], w2_s[:, k, :], o1[:, k, :], start=k == 0, stop=k == K1 - 1)
                    mm.then_inc(sums_done, 1)
                    pe.wait_ge(act_ready, 5 * c + 3)
                    for m in range(K3):
                        pe.matmul(bank[4 + m][:], w3_s[:, m * P:(m + 1) * P], o2[:], start=True, stop=True
                                  ).then_inc(sums_done, 1)
                    pe.wait_ge(act_ready, 5 * c + 5)
                    for t in range(TC):
                        for k in range(K3):
                            mm = pe.matmul(bank[t][:], o3[:, k, t * P:(t + 1) * P], w4_s[:, k, :],
                                           start=k == 0, stop=k == K3 - 1)
                        mm.then_inc(rows_done, 1)


def build(nc, x, adj, adj_t, w, a1, a2, w1_t, b1, w2_t, b2, w3_t, b3, w4_t, b4, out):
    src_rows = nc.dram_tensor("src_rows", (H, N), F32, kind="Internal").ap()
    dst_top = nc.dram_tensor("dst_top", (H, 1), F32, kind="Internal").ap()
    x1_store = nc.dram_tensor("x1_store", (N, F), F32, kind="Internal").ap()
    with ExitStack() as ctx:
        def sb(name, shape, dt=F32, within=ctx):
            return within.enter_context(nc.sbuf_tensor(name, shape, dt))

        bank = [ctx.enter_context(nc.psum_tensor(f"bank{k}", [P, 512], F32)) for k in range(8)]
        ident = sb("ident", [P, P])
        make_identity(nc, ident)
        rstd = sb("rstd", [P, T])
        nmr = sb("nmr", [P, T])
        e = sb("e", [P, T, 2 * H])
        smooth = ctx.enter_context(ExitStack())
        G = smooth.enter_context(nc.sbuf_tensor("G", [P, T, F], F32, side="right"))
        smooth_features(nc, bank, G, x, adj, adj_t)
        mask = sb("mask", [P, T, N], U8)
        wh = sb("wh", [P, T, H, HE])
        with nc.sbuf_tensor("x1", [P, T, F], F32) as x1:
            spread_features(nc, bank, G, x1, mask, rstd, nmr, x, adj_t)
            smooth.close()
            project_heads(nc, bank, x1, rstd, nmr, wh, e, ident, w, a1, a2, src_rows, dst_top, x1_store)
        fac = {f: sb(f"fac_{f}", [P, T, H]) for f in "ABCD"}
        neg_d = sb("neg_d", [P, T, H])
        md = sb("md", [P, T, H, HE])
        edge_factors(nc, bank, wh, e, mask, fac, neg_d, md, dst_top)
        attend(nc, bank, wh, mask, fac, neg_d, md, src_rows)
        feed_forward(nc, bank, wh, ident, x1_store, w1_t, b1, w2_t, b2, w3_t, b3, w4_t, b4, out)


_WEIGHTS = ("a1", "a2", "W1", "b1", "W2", "b2", "W3", "b3", "W4", "b4")


def kernel(x, adj, L1_gnn_W, **weights):
    import numpy as np
    import concourse.bacc as bacc
    from concourse.bass_utils import run_bass_kernel_spmd

    nc = bacc.Bacc("TRN2", target_bir_lowering=False, num_devices=1)
    arrays = {"x": x, "adj": adj, "adj_t": np.asarray(adj).T, "w": L1_gnn_W}
    for name in _WEIGHTS:
        a = np.asarray(weights[f"L1_gnn_{name}"])
        if name in ("b1", "b2", "b3"):
            a = a.reshape(-1, P)
        arrays[name] = a.T if a.ndim == 2 and name[0] != "a" else a
    arrays = {name: np.ascontiguousarray(a) for name, a in arrays.items()}
    aps = [nc.dram_tensor(name, a.shape, mybir.dt.from_np(a.dtype), kind="ExternalInput").ap()
           for name, a in arrays.items()]
    out = nc.dram_tensor("out", (N, F), F32, kind="ExternalOutput").ap()
    build(nc, *aps, out)
    return run_bass_kernel_spmd(nc, [arrays], core_ids=[0]).results[0]["out"]
```

```python
from contextlib import ExitStack

import concourse.bass as bass
from concourse import mybir

F32 = mybir.dt.float32
F32R = mybir.dt.float32r
U8 = mybir.dt.uint8
ALU = mybir.AluOpType
ACT = mybir.ActivationFunctionType
AX_X = mybir.AxisListType.X

P = 128
N = 2048
F = 512
T = N // P
H = 8
HD = F // H
HE = HD + 1
KC = F // P
G8 = 8
GW = G8 * P
EPS = 1e-5
SLOPE = 0.2
TINY = 1e-30


def refine_rsqrt(v, chain, count, d, root, y, tmp):
    v.reciprocal(y, root).then_inc(chain, 1)
    v.wait_ge(chain, count + 1)
    v.tensor_tensor(tmp, y, y, ALU.mult).then_inc(chain, 1)
    v.wait_ge(chain, count + 2)
    v.tensor_tensor(tmp, tmp, d, ALU.mult).then_inc(chain, 1)
    v.wait_ge(chain, count + 3)
    v.tensor_scalar(tmp, tmp, -0.5, 1.5, ALU.mult, ALU.add).then_inc(chain, 1)
    v.wait_ge(chain, count + 4)
    v.tensor_tensor(y, y, tmp, ALU.mult).then_inc(chain, 1)
    v.wait_ge(chain, count + 5)


def split_product(pe, acc, hi, lo, rhs_hi, rhs_lo, first):
    pe.matmul(acc, hi, rhs_hi, start=first, stop=False, skip_group_check=True)
    pe.matmul(acc, hi, rhs_lo, start=False, stop=False, skip_group_check=True)
    return pe.matmul(acc, lo, rhs_hi, start=False, stop=True, skip_group_check=True)


def make_identity(nc, ident):
    with nc.semaphore("ident_zeroed") as zeroed, nc.Block() as block:
        @block.gpsimd
        def _(g):
            g.memset(ident[:], 0.0).then_inc(zeroed, 1)
            g.wait_ge(zeroed, 1)
            g.affine_select(out=ident[:], in_=ident[:], compare_op=ALU.not_equal, fill=1.0, base=0,
                            pattern=[[-1, P]], channel_multiplier=1)


def smooth_features(nc, bank, G, x, adj, adj_t):
    with ExitStack() as ctx:
        def sb(name, shape, dt=F32):
            return ctx.enter_context(nc.sbuf_tensor(name, shape, dt))

        def sem(name):
            return ctx.enter_context(nc.semaphore(name))

        h = sb("l0_h", [P, T, F])
        sum_a = sb("l0_sum_a", [P, 2, GW])
        sum_b = sb("l0_sum_b", [P, T, GW])
        rows_t = sb("l0_rows_t", [P, 2, N])
        s_hi = sb("l0_s_hi", [P, 2, GW], F32R)
        s_lo = sb("l0_s_lo", [P, 2, GW], F32R)
        x_hi = sb("l0_x_hi", [P, 2, F], F32R)
        x_lo = sb("l0_x_lo", [P, 2, F], F32R)
        stats = sb("l0_stats", [P, T, 6])
        mv = sb("l0_mv", [P, T, 2])
        var = sb("l0_var", [P, T])
        root = sb("l0_root", [P, T])
        rstd = sb("l0_rstd", [P, T])
        nmr = sb("l0_nmr", [P, T])
        tmp = sb("l0_tmp", [P, T])
        part = sb("l0_part", [P, 2, 2])
        deg = sb("l0_deg", [P, T, 1])
        degc = sb("l0_degc", [P, T, 1])
        droot = sb("l0_droot", [P, T, 1])
        y = sb("l0_y", [P, T, 1])
        ytmp = sb("l0_ytmp", [P, T, 1])
        dinv = sb("l0_dinv", [P, T, 1])
        hdinv = sb("l0_hdinv", [P, T, 1])

        x_loaded = sem("l0_x_loaded")
        rows_loaded = [sem(f"l0_rows_loaded{b}") for b in range(2)]
        ln_chain = sem("l0_ln_chain")
        var_ready = sem("l0_var_ready")
        ln_root = sem("l0_ln_root")
        norm_ready = sem("l0_norm_ready")
        h_ready = sem("l0_h_ready")
        summed = sem("l0_summed")
        deg_chain = sem("l0_deg_chain")
        deg_ready = sem("l0_deg_ready")
        root_ready = sem("l0_root_ready")
        hi_ready = sem("l0_hi_ready")
        lo_ready = sem("l0_lo_ready")
        x_chain = sem("l0_x_chain")
        x_ready = sem("l0_x_ready")
        slot_free = sem("l0_slot_free")
        acc_done = sem("l0_acc_done")
        base_ready = sem("l0_base_ready")
        g_done = sem("l0_g_done")
        DEG = 9

        with nc.Block() as block:
            @block.sync
            def _(sp):
                sp.dma_start(h[:], x.rearrange("(t p) f -> p t f", p=P)).then_inc(x_loaded, 16)

                def load(i, b):
                    rows = bass.ds(i * P, P)
                    sp.dma_start(rows_t[:, b, :], adj_t[rows, :]).then_inc(rows_loaded[b], 16)
                    sp.dma_start(sum_a[:, b, :], adj[rows, 0:GW]).then_inc(rows_loaded[b], 16)
                    sp.dma_start(sum_b[:, i, :], adj[rows, GW:N]).then_inc(rows_loaded[b], 16)

                load(0, 0)
                load(1, 1)
                with sp.Fori(1, T // 2) as j:
                    for b in range(2):
                        sp.wait_ge(summed, 4 * j + 2 * b - 2)
                        sp.wait_ge(lo_ready, 2 * j + b - 1)
                        load(2 * j + b, b)

            @block.vector
            def _(v):
                v.wait_ge(x_loaded, 16)
                with v.Fori(0, T) as t:
                    v.bn_stats(stats[:, t, :], h[:, t, :]).then_inc(ln_chain, 1)
                v.wait_ge(ln_chain, T)
                for t in range(T):
                    v.bn_aggr(mv[:, t, :], stats[:, t, :]).then_inc(ln_chain, 1)
                v.wait_ge(ln_chain, 2 * T)
                v.tensor_scalar(var[:], mv[:, :, 1], EPS, None, ALU.add).then_inc(var_ready, 1)
                v.wait_ge(ln_root, 1)
                refine_rsqrt(v, ln_chain, 2 * T, var[:], root[:], rstd[:], tmp[:])
                v.scalar_tensor_tensor(out=nmr[:], in0=mv[:, :, 0], scalar=-1.0, in1=rstd[:],
                                       op0=ALU.mult, op1=ALU.mult).then_inc(norm_ready, 1)

                def x_parts(i, b, s):
                    v.wait_ge(slot_free, s + 1)
                    v.tensor_scalar(x_hi[:, b, :], h[:, i, :], dinv[:, i, :], None,
                                    ALU.mult).then_inc(x_chain, 1)
                    v.wait_ge(x_chain, s + 1)
                    v.scalar_tensor_tensor(out=x_lo[:, b, :], in0=h[:, i, :], scalar=dinv[:, i, :],
                                           in1=x_hi[:, b, :].bitcast(F32), op0=ALU.mult,
                                           op1=ALU.subtract).then_inc(x_ready, 1)

                with v.Fori(0, T // 2) as j:
                    for b in range(2):
                        i = 2 * j + b
                        c = DEG * i
                        v.wait_ge(rows_loaded[b], 48 * j + 48)
                        v.scalar_tensor_tensor(out=sum_a[:, b, :], in0=rows_t[:, b, 0:GW], scalar=1.0,
                                               in1=sum_a[:, b, :], op0=ALU.mult, op1=ALU.add,
                                               accum_out=part[:, b, 0:1]).then_inc(summed, 1)
                        v.scalar_tensor_tensor(out=sum_b[:, i, :], in0=rows_t[:, b, GW:N], scalar=1.0,
                                               in1=sum_b[:, i, :], op0=ALU.mult, op1=ALU.add,
                                               accum_out=part[:, b, 1:2]).then_inc(summed, 1)
                        v.wait_ge(summed, 2 * i + 2)
                        v.tensor_tensor(deg[:, i, :], part[:, b, 0:1], part[:, b, 1:2],
                                        ALU.add).then_inc(deg_chain, 1)
                        v.wait_ge(deg_chain, c + 1)
                        v.tensor_scalar(deg[:, i, :], deg[:, i, :], 0.5, 1.0, ALU.mult,
                                        ALU.add).then_inc(deg_chain, 1)
                        v.wait_ge(deg_chain, c + 2)
                        v.tensor_scalar(degc[:, i, :], deg[:, i, :], TINY, None,
                                        ALU.max).then_inc(deg_ready, 1)
                        v.wait_ge(root_ready, i + 1)
                        refine_rsqrt(v, deg_chain, c + 2, degc[:, i, :], droot[:, i, :], y[:, i, :],
                                     ytmp[:, i, :])
                        v.scalar_tensor_tensor(out=dinv[:, i, :], in0=deg[:, i, :], scalar=0.0,
                                               in1=y[:, i, :], op0=ALU.is_gt,
                                               op1=ALU.mult).then_inc(deg_chain, 1)
                        v.wait_ge(deg_chain, c + 8)
                        v.tensor_scalar(hdinv[:, i, :], dinv[:, i, :], 0.5, None,
                                        ALU.mult).then_inc(deg_chain, 1)
                        v.wait_ge(h_ready, i + 1)
                        x_parts(i, b, i)
                v.wait_ge(deg_chain, DEG * T)

                def write_g(g):
                    with v.Fori(0, G8) as k:
                        v.tensor_scalar(G[:, G8 * g + k, :], h[:, G8 * g + k, :], dinv[:, G8 * g + k, :],
                                        dinv[:, G8 * g + k, :], ALU.mult, ALU.mult).then_inc(base_ready, 1)
                    v.wait_ge(base_ready, G8 * (g + 1))
                    for k in range(G8):
                        n = G8 * g + k
                        v.wait_ge(acc_done, n + 1)
                        v.scalar_tensor_tensor(out=G[:, n, :], in0=bank[k][:], scalar=hdinv[:, n, :],
                                               in1=G[:, n, :], op0=ALU.mult, op1=ALU.add).then_inc(g_done, 1)

                write_g(0)
                with v.Fori(0, T // 2) as j:
                    for b in range(2):
                        x_parts(2 * j + b, b, T + 2 * j + b)
                write_g(1)

            @block.scalar
            def _(a):
                a.wait_ge(var_ready, 1)
                a.activation(root[:], var[:], ACT.Sqrt).then_inc(ln_root, 1)
                a.wait_ge(norm_ready, 1)
                with a.Fori(0, T) as t:
                    a.activation(h[:, t, :], h[:, t, :], ACT.Relu, bias=nmr[:, bass.ds(t, 1)],
                                 scale=rstd[:, bass.ds(t, 1)]).then_inc(h_ready, 1)
                with a.Fori(0, T // 2) as j:
                    for b in range(2):
                        i = 2 * j + b
                        a.wait_ge(deg_ready, i + 1)
                        a.activation(droot[:, i, :], degc[:, i, :], ACT.Sqrt).then_inc(root_ready, 1)
                        a.wait_ge(slot_free, i + 1)
                        a.activation(s_hi[:, b, :], sum_a[:, b, :], ACT.Copy).then_inc(hi_ready, 1)
                with a.Fori(0, T // 2) as j:
                    for b in range(2):
                        i = 2 * j + b
                        a.wait_ge(slot_free, T + i + 1)
                        a.activation(s_hi[:, b, :], sum_b[:, i, :], ACT.Copy).then_inc(hi_ready, 1)

            @block.gpsimd
            def _(g):
                with g.Fori(0, T // 2) as j:
                    for b in range(2):
                        g.wait_ge(hi_ready, 2 * j + b + 1)
                        g.tensor_tensor(s_lo[:, b, :], sum_a[:, b, :], s_hi[:, b, :].bitcast(F32),
                                        ALU.subtract).then_inc(lo_ready, 1)
                with g.Fori(0, T // 2) as j:
                    for b in range(2):
                        g.wait_ge(hi_ready, T + 2 * j + b + 1)
                        g.tensor_tensor(s_lo[:, b, :], sum_b[:, 2 * j + b, :], s_hi[:, b, :].bitcast(F32),
                                        ALU.subtract).then_inc(lo_ready, 1)

            @block.tensor
            def _(pe):
                pe.sem_inc(slot_free, 2)

                def products(s, b, g, first, last):
                    pe.wait_ge(lo_ready, s + 1)
                    pe.wait_ge(x_ready, s + 1)
                    for k in range(G8):
                        if first and g == 1:
                            pe.wait_ge(g_done, k + 1)
                        cols = slice(k * P, (k + 1) * P)
                        mm = split_product(pe, bank[k][:], s_hi[:, b, cols], s_lo[:, b, cols],
                                           x_hi[:, b, :], x_lo[:, b, :], first)
                        if last:
                            mm.then_inc(acc_done, 1)
                    if not last:
                        mm.then_inc(slot_free, 1)

                for g in range(2):
                    products(T * g, 0, g, True, False)
                    with pe.Fori(0, T // 2 - 1) as j:
                        products(T * g + 2 * j + 1, 1, g, False, False)
                        products(T * g + 2 * j + 2, 0, g, False, False)
                    products(T * g + T - 1, 1, g, False, True)
                    if g == 0:
                        pe.wait_ge(acc_done, G8)
                        pe.sem_inc(slot_free, 1)


def spread_features(nc, bank, G, x1, mask, rstd, nmr, x, adj_t):
    with ExitStack() as ctx:
        def sb(name, shape, dt=F32):
            return ctx.enter_context(nc.sbuf_tensor(name, shape, dt))

        def sem(name):
            return ctx.enter_context(nc.semaphore(name))

        rows = sb("l1_rows", [P, 4, GW])
        a_hi = sb("l1_a_hi", [P, 2, GW], F32R)
        a_lo = sb("l1_a_lo", [P, 2, GW], F32R)
        g_hi = sb("l1_g_hi", [P, 2, F], F32R)
        g_lo = sb("l1_g_lo", [P, 2, F], F32R)
        stats = sb("l1_stats", [P, T, 6])
        mv = sb("l1_mv", [P, T, 2])
        var = sb("l1_var", [P, T])
        root = sb("l1_root", [P, T])
        tmp = sb("l1_tmp", [P, T])

        x_loaded = sem("l1_x_loaded")
        rows_loaded = [sem(f"l1_rows_loaded{b}") for b in range(4)]
        hi_ready = sem("l1_hi_ready")
        lo_ready = sem("l1_lo_ready")
        g_chain = sem("l1_g_chain")
        g_ready = sem("l1_g_ready")
        mask_done = sem("l1_mask_done")
        slot_free = sem("l1_slot_free")
        acc_done = sem("l1_acc_done")
        x1_done = sem("l1_x1_done")
        ln_chain = sem("l1_ln_chain")
        var_ready = sem("l1_var_ready")
        ln_root = sem("l1_ln_root")

        with nc.Block() as block:
            @block.sync
            def _(sp):
                def load(g, i, r):
                    sp.dma_start(rows[:, r, :], adj_t[bass.ds(i * P, P), g * GW:(g + 1) * GW]
                                 ).then_inc(rows_loaded[r], 16)

                for r in range(4):
                    load(0, r, r)
                sp.dma_start(x1[:], x.rearrange("(t p) f -> p t f", p=P)).then_inc(x_loaded, 16)
                for g in range(2):
                    with sp.Fori(1 - g, T // 4) as j:
                        for r in range(4):
                            sp.wait_ge(lo_ready, T * g + 4 * j + r - 3)
                            sp.wait_ge(mask_done, T * g + 4 * j + r - 3)
                            load(g, 4 * j + r, r)

            def steps(eng, body):
                for g in range(2):
                    with eng.Fori(0, T // 4) as j:
                        for r in range(4):
                            body(g, 4 * j + r, r, T * g + 4 * j + r, 4 * g + j)

            @block.scalar
            def _(a):
                def cut_hi(g, i, r, s, turn):
                    a.wait_ge(rows_loaded[r], 16 * turn + 16)
                    a.wait_ge(slot_free, s + 1)
                    a.activation(a_hi[:, r % 2, :], rows[:, r, :], ACT.Copy).then_inc(hi_ready, 1)
                steps(a, cut_hi)
                a.wait_ge(var_ready, 1)
                a.activation(root[:], var[:], ACT.Sqrt).then_inc(ln_root, 1)

            @block.vector
            def _(v):
                def cut(g, i, r, s, turn):
                    b = r % 2
                    v.wait_ge(slot_free, s + 1)
                    v.tensor_copy(g_hi[:, b, :], G[:, i, :]).then_inc(g_chain, 1)
                    v.wait_ge(g_chain, s + 1)
                    v.tensor_tensor(g_lo[:, b, :], G[:, i, :], g_hi[:, b, :].bitcast(F32),
                                    ALU.subtract).then_inc(g_ready, 1)
                    v.wait_ge(hi_ready, s + 1)
                    v.tensor_tensor(a_lo[:, b, :], rows[:, r, :], a_hi[:, b, :].bitcast(F32),
                                    ALU.subtract).then_inc(lo_ready, 1)
                    v.tensor_scalar(mask[:, i, g * GW:(g + 1) * GW], rows[:, r, :], 0.0, None,
                                    ALU.is_gt).then_inc(mask_done, 1)

                def add_y(g):
                    for k in range(G8):
                        n = G8 * g + k
                        v.wait_ge(acc_done, n + 1)
                        v.tensor_tensor(x1[:, n, :], bank[k][:], x1[:, n, :], ALU.add).then_inc(x1_done, 1)

                def stats_of(g):
                    v.wait_ge(x1_done, G8 * (g + 1))
                    with v.Fori(0, G8) as k:
                        v.bn_stats(stats[:, G8 * g + k, :], x1[:, G8 * g + k, :]).then_inc(ln_chain, 1)

                with v.Fori(0, T // 4) as j:
                    for r in range(4):
                        cut(0, 4 * j + r, r, 4 * j + r, j)
                v.wait_ge(x_loaded, 16)
                add_y(0)
                with v.Fori(0, T // 4) as j:
                    for r in range(4):
                        cut(1, 4 * j + r, r, T + 4 * j + r, 4 + j)
                stats_of(0)
                add_y(1)
                stats_of(1)
                v.wait_ge(ln_chain, T)
                for t in range(T):
                    v.bn_aggr(mv[:, t, :], stats[:, t, :]).then_inc(ln_chain, 1)
                v.wait_ge(ln_chain, 2 * T)
                v.tensor_scalar(var[:], mv[:, :, 1], EPS, None, ALU.add).then_inc(var_ready, 1)
                v.wait_ge(ln_root, 1)
                refine_rsqrt(v, ln_chain, 2 * T, var[:], root[:], rstd[:], tmp[:])
                v.scalar_tensor_tensor(out=nmr[:], in0=mv[:, :, 0], scalar=-1.0, in1=rstd[:],
                                       op0=ALU.mult, op1=ALU.mult)

            @block.tensor
            def _(pe):
                pe.sem_inc(slot_free, 2)

                def products(s, b, g, first, last):
                    pe.wait_ge(g_ready, s + 1)
                    pe.wait_ge(lo_ready, s + 1)
                    for k in range(G8):
                        if first and g == 1:
                            pe.wait_ge(x1_done, k + 1)
                        cols = slice(k * P, (k + 1) * P)
                        mm = split_product(pe, bank[k][:], a_hi[:, b, cols], a_lo[:, b, cols],
                                           g_hi[:, b, :], g_lo[:, b, :], first)
                        if last:
                            mm.then_inc(acc_done, 1)
                    if not last:
                        mm.then_inc(slot_free, 1)

                for g in range(2):
                    products(T * g, 0, g, True, False)
                    with pe.Fori(0, T // 2 - 1) as j:
                        products(T * g + 2 * j + 1, 1, g, False, False)
                        products(T * g + 2 * j + 2, 0, g, False, False)
                    products(T * g + T - 1, 1, g, False, True)
                    if g == 0:
                        pe.wait_ge(acc_done, G8)
                        pe.sem_inc(slot_free, 1)


def project_heads(nc, bank, x1, rstd, nmr, wh, e, ident, w, a1, a2, src_rows, dst_range, x1_store):
    with ExitStack() as ctx:
        def sb(name, shape, dt=F32):
            return ctx.enter_context(nc.sbuf_tensor(name, shape, dt))

        def sem(name):
            return ctx.enter_context(nc.semaphore(name))

        w_f = sb("l2_w", [P, KC, H, HD])
        w_hi = sb("l2_w_hi", [P, KC, F], F32R)
        w_lo = sb("l2_w_lo", [P, KC, F], F32R)
        a_b = sb("l2_a", [P, 2, F])
        h2 = sb("l2_h", [P, 2, F])
        ht_hi = sb("l2_ht_hi", [P, 2, F], F32R)
        ht_lo = sb("l2_ht_lo", [P, 2, F], F32R)
        prod = sb("l2_prod", [P, 2, 2, F])
        e_t = sb("l2_e_t", [2 * H, N])
        top = sb("l2_top", [2 * H, 1])

        loaded = sem("l2_loaded")
        w_chain = sem("l2_w_chain")
        w_ready = sem("l2_w_ready")
        ones_ready = sem("l2_ones_ready")
        h_ready = sem("l2_h_ready")
        turned = sem("l2_turned")
        hi_ready = sem("l2_hi_ready")
        lo_ready = sem("l2_lo_ready")
        acc_done = sem("l2_acc_done")
        wh_ready = sem("l2_wh_ready")
        prod_ready = sem("l2_prod_ready")
        e_ready = sem("l2_e_ready")
        e_turned = sem("l2_e_turned")
        e_copied = sem("l2_e_copied")
        top_ready = sem("l2_top_ready")
        stored = sem("l2_stored")
        top_stored = sem("l2_top_stored")
        x1_stored = sem("l2_x1_stored")

        with nc.Block() as block:
            @block.sync
            def _(sp):
                sp.dma_start(x1_store.rearrange("(t p) f -> p t f", p=P), x1[:]).then_inc(x1_stored, 16)
                for k in range(KC):
                    sp.dma_start(w_f[:, k, :, :], w[:, k * P:(k + 1) * P, :].rearrange("h p d -> p h d")
                                 ).then_inc(loaded, 16)
                for n, a in enumerate((a1, a2)):
                    row = a.rearrange("h d -> (h d)").rearrange("(o f) -> o f", o=1)
                    sp.dma_start(a_b[:, n, :], row.to_broadcast([P, F])).then_inc(loaded, 16)
                sp.wait_ge(e_copied, 4)
                sp.dma_start(src_rows, e_t[0:H, :]).then_inc(stored, 16)
                sp.wait_ge(top_ready, 1)
                sp.dma_start(dst_range, top[H:2 * H, :]).then_inc(top_stored, 16)
                sp.wait_ge(stored, 16)
                sp.wait_ge(top_stored, 16)
                sp.wait_ge(x1_stored, 16)

            @block.scalar
            def _(a):
                def normalise(t, b):
                    a.wait_ge(turned, t + 1)
                    a.activation(h2[:, b, :], x1[:, t, :], ACT.Relu, bias=nmr[:, bass.ds(t, 1)],
                                 scale=rstd[:, bass.ds(t, 1)]).then_inc(h_ready, 1)

                def tile(t, b, last):
                    a.wait_ge(turned, t + 3)
                    a.wait_ge(acc_done, t + 1)
                    a.activation(ht_hi[:, b, :], bank[b][:], ACT.Copy).then_inc(hi_ready, 1)
                    if not last:
                        normalise(t + 1, 1 - b)
                    a.wait_ge(acc_done, t + 3)
                    a.activation(wh[:, t, :, 0:HD], bank[2 + b][:].rearrange("p (h d) -> p h d", h=H),
                                 ACT.Copy).then_inc(wh_ready, 1)

                a.sem_inc(wh_ready, 2)
                normalise(0, 0)
                with a.Fori(0, T // 2 - 1) as j:
                    for b in range(2):
                        tile(2 * j + b, b, False)
                tile(T - 2, 0, False)
                tile(T - 1, 1, True)

            @block.vector
            def _(v):
                v.memset(wh[:, :, :, HD:HE], 1.0).then_inc(ones_ready, 1)
                v.wait_ge(loaded, 16 * (KC + 2))
                v.tensor_copy(w_hi[:], w_f[:].rearrange("p k h d -> p k (h d)")).then_inc(w_chain, 1)
                v.wait_ge(w_chain, 1)
                v.tensor_tensor(w_lo[:], w_f[:].rearrange("p k h d -> p k (h d)"), w_hi[:].bitcast(F32),
                                ALU.subtract).then_inc(w_ready, 1)
                v.sem_inc(e_ready, 4)
                with v.Fori(0, T // 2) as j:
                    for b in range(2):
                        t = 2 * j + b
                        v.wait_ge(hi_ready, t + 1)
                        v.tensor_tensor(ht_lo[:, b, :], bank[b][:], ht_hi[:, b, :].bitcast(F32),
                                        ALU.subtract).then_inc(lo_ready, 1)
                        v.wait_ge(wh_ready, t + 3)
                        v.wait_ge(e_ready, 2 * t + 2)
                        for n in range(2):
                            v.tensor_tensor(prod[:, b, n, :].rearrange("p (h d) -> p h d", h=H),
                                            wh[:, t, :, 0:HD],
                                            a_b[:, n, :].rearrange("p (h d) -> p h d", h=H),
                                            ALU.mult).then_inc(prod_ready, 1)
                        for n in range(2):
                            v.wait_ge(prod_ready, 2 * t + n + 1)
                            v.tensor_reduce(e[:, t, n * H:(n + 1) * H],
                                            prod[:, b, n, :].rearrange("p (h d) -> p h d", h=H),
                                            AX_X, ALU.add).then_inc(e_ready, 1)
                for q in range(4):
                    v.wait_ge(e_turned, q + 1)
                    v.tensor_copy(e_t[:, q * 512:(q + 1) * 512], bank[4 + q][0:2 * H, :]).then_inc(e_copied, 1)
                v.wait_ge(e_copied, 4)
                v.tensor_reduce(top[:], e_t[:], AX_X, ALU.max).then_inc(top_ready, 1)

            @block.tensor
            def _(pe):
                pe.sem_inc(turned, 2)
                pe.sem_inc(acc_done, 2)
                pe.wait_ge(w_ready, 1)

                def turn(t, b):
                    pe.wait_ge(h_ready, t + 1)
                    for k in range(KC):
                        cols = slice(k * P, (k + 1) * P)
                        mm = pe.transpose(bank[b][:, cols], h2[:, b, cols], ident[:])
                    mm.then_inc(turned, 1)

                def tile(t, b, last):
                    if not last:
                        turn(t + 1, 1 - b)
                    pe.wait_ge(lo_ready, t + 1)
                    pe.wait_ge(wh_ready, t + 1)
                    for k in range(KC):
                        cols = slice(k * P, (k + 1) * P)
                        mm = split_product(pe, bank[2 + b][:], ht_hi[:, b, cols], ht_lo[:, b, cols],
                                           w_hi[:, k, :], w_lo[:, k, :], k == 0)
                    mm.then_inc(acc_done, 1)

                turn(0, 0)
                with pe.Fori(0, T // 2 - 1) as j:
                    for b in range(2):
                        tile(2 * j + b, b, False)
                tile(T - 2, 0, False)
                tile(T - 1, 1, True)
                pe.wait_ge(e_ready, 2 * T + 4)
                for t in range(T):
                    mm = pe.transpose(bank[4 + t // 4][0:2 * H, (t % 4) * P:(t % 4 + 1) * P], e[:, t, :], ident[:])
                    if t % 4 == 3:
                        mm.then_inc(e_turned, 1)


def edge_factors(nc, bank, wh, e, mask, fac, neg_d, md, dst_top):
    with ExitStack() as ctx:
        def sb(name, shape, dt=F32):
            return ctx.enter_context(nc.sbuf_tensor(name, shape, dt))

        def sem(name):
            return ctx.enter_context(nc.semaphore(name))

        GT = 4
        NG = T // GT
        HW = H // 2 * HE
        top = sb("l3_top", [P, 1, H])
        t1 = sb("l3_t1", [P, T, H])
        t2 = sb("l3_t2", [P, T, H])
        t3 = sb("l3_t3", [P, T, H])
        cw = sb("l3_cw", [P, 2, H, HE])
        cw_hi = sb("l3_cw_hi", [P, 2, 2, HW], F32R)
        cw_lo = sb("l3_cw_lo", [P, 2, 2, HW], F32R)
        m_r = sb("l3_mask_r", [P, 2, GT * P], F32R)

        loaded = sem("l3_loaded")
        chain = sem("l3_chain")
        args_ready = sem("l3_args_ready")
        fac_ready = sem("l3_fac_ready")
        cw_ready = sem("l3_cw_ready")
        cw_hi_ready = sem("l3_cw_hi_ready")
        cw_lo_ready = sem("l3_cw_lo_ready")
        mask_ready = sem("l3_mask_ready")
        slot_free = sem("l3_slot_free")
        acc_done = sem("l3_acc_done")
        md_done = sem("l3_md_done")

        with nc.Block() as block:
            @block.sync
            def _(sp):
                sp.dma_start(top[:, 0, :], dst_top.rearrange("h o -> o h").to_broadcast([P, H])
                             ).then_inc(loaded, 16)

            @block.vector
            def _(v):
                v.wait_ge(loaded, 16)
                src, dst = e[:, :, 0:H], e[:, :, H:2 * H]
                top_t = top[:].to_broadcast([P, T, H])
                v.tensor_tensor(t1[:], dst, top_t, ALU.subtract).then_inc(args_ready, 1)
                v.tensor_tensor(t2[:], src, top_t, ALU.add).then_inc(chain, 1)
                v.tensor_scalar(neg_d[:], dst, -1.0, None, ALU.mult).then_inc(chain, 1)
                v.wait_ge(chain, 2)
                v.tensor_scalar(t3[:], t2[:], 1.0 - SLOPE, 0.0, ALU.mult, ALU.min).then_inc(args_ready, 1)
                v.wait_ge(args_ready, 2)
                v.tensor_scalar(t2[:], t2[:], SLOPE - 1.0, 0.0, ALU.mult, ALU.min).then_inc(args_ready, 1)
                v.wait_ge(fac_ready, 4)
                for g in range(NG):
                    with v.Fori(0, T // 2) as j:
                        for b in range(2):
                            i = 2 * j + b
                            s = T * g + i
                            v.wait_ge(slot_free, s + 1)
                            v.tensor_tensor(cw[:, b, :, :], wh[:, i, :, :],
                                            fac["C"][:, i, :].unsqueeze(2).to_broadcast([P, H, HE]),
                                            ALU.mult).then_inc(cw_ready, 1)
                            v.wait_ge(cw_hi_ready, s + 1)
                            v.tensor_tensor(cw_lo[:, b, :, :].rearrange("p a c -> p (a c)"),
                                            cw[:, b, :, :].rearrange("p h e -> p (h e)"),
                                            cw_hi[:, b, :, :].rearrange("p a c -> p (a c)").bitcast(F32),
                                            ALU.subtract).then_inc(cw_lo_ready, 1)
                    for k in range(2 * GT):
                        n, half = GT * g + k // 2, slice(k % 2 * H // 2, (k % 2 + 1) * H // 2)
                        v.wait_ge(acc_done, 2 * GT * g + k + 1)
                        v.tensor_tensor(md[:, n, half, :],
                                        bank[k][:, 0:HW].rearrange("p (h e) -> p h e", e=HE),
                                        fac["D"][:, n, half].unsqueeze(2).to_broadcast([P, H // 2, HE]),
                                        ALU.mult).then_inc(md_done, 1)

            @block.scalar
            def _(a):
                a.wait_ge(args_ready, 1)
                a.activation(fac["A"][:], t1[:], ACT.Exp).then_inc(fac_ready, 1)
                a.activation(fac["C"][:], t1[:], ACT.Exp, scale=SLOPE).then_inc(fac_ready, 1)
                a.wait_ge(args_ready, 3)
                a.activation(fac["B"][:], t3[:], ACT.Exp).then_inc(fac_ready, 1)
                a.activation(fac["D"][:], t2[:], ACT.Exp).then_inc(fac_ready, 1)
                for g in range(NG):
                    with a.Fori(0, T // 2) as j:
                        for b in range(2):
                            i = 2 * j + b
                            s = T * g + i
                            a.wait_ge(slot_free, s + 1)
                            a.activation(m_r[:, b, :], mask[:, i, GT * g * P:GT * (g + 1) * P],
                                         ACT.Copy).then_inc(mask_ready, 1)
                            a.wait_ge(cw_ready, s + 1)
                            a.activation(cw_hi[:, b, :, :].rearrange("p a c -> p (a c)"),
                                         cw[:, b, :, :].rearrange("p h e -> p (h e)"),
                                         ACT.Copy).then_inc(cw_hi_ready, 1)

            @block.tensor
            def _(pe):
                pe.sem_inc(slot_free, 2)

                def products(s, b, g, first, last):
                    pe.wait_ge(mask_ready, s + 1)
                    pe.wait_ge(cw_lo_ready, s + 1)
                    for k in range(2 * GT):
                        if first and g:
                            pe.wait_ge(md_done, 2 * GT * (g - 1) + k + 1)
                        acc = bank[k][:, 0:HW]
                        blk = m_r[:, b, k // 2 * P:(k // 2 + 1) * P]
                        pe.matmul(acc, blk, cw_hi[:, b, k % 2, :], start=first, stop=False,
                                  skip_group_check=True)
                        mm = pe.matmul(acc, blk, cw_lo[:, b, k % 2, :], start=False, stop=True,
                                       skip_group_check=True)
                        if last:
                            mm.then_inc(acc_done, 1)
                    if not last:
                        mm.then_inc(slot_free, 1)

                for g in range(NG):
                    products(T * g, 0, g, True, False)
                    with pe.Fori(0, T // 2 - 1) as j:
                        products(T * g + 2 * j + 1, 1, g, False, False)
                        products(T * g + 2 * j + 2, 0, g, False, False)
                    products(T * g + T - 1, 1, g, False, True)
                    if g < NG - 1:
                        pe.wait_ge(acc_done, 2 * GT * (g + 1))
                        pe.sem_inc(slot_free, 1)


def attend(nc, bank, wh, mask, fac, neg_d, md, src_rows):
    with ExitStack() as ctx:
        def sb(name, shape, dt=F32):
            return ctx.enter_context(nc.sbuf_tensor(name, shape, dt))

        def sem(name):
            return ctx.enter_context(nc.semaphore(name))

        PW = 2 * HE
        QUAD = 4
        NQ = T // QUAD
        src = sb("l4_src", [P, 2, N])
        q = sb("l4_q", [P, 2 * QUAD, GW], F32R)
        whole = sb("l4_whole", [P, T, HE])
        parts = sb("l4_parts", [P, 2, T, 2 * PW], F32R)
        o = sb("l4_o", [P, 2, G8, 2 * PW])
        rden = sb("l4_rden", [P, 2, G8, 1])

        src_loaded = [sem(f"l4_src_loaded{b}") for b in range(2)]
        whole_ready = sem("l4_whole_ready")
        part_hi = sem("l4_part_hi")
        part_lo = sem("l4_part_lo")
        q_ready = sem("l4_q_ready")
        acc_done = sem("l4_acc_done")
        acc_free = sem("l4_acc_free")
        scaled = sem("l4_scaled")
        o_free = sem("l4_o_free")
        rden_ready = sem("l4_rden_ready")
        dividing = sem("l4_dividing")
        EARLY = 2 * G8
        STEPS = 5

        def heads(eng, body):
            body(0, 0, 0, True, False)
            with eng.Fori(0, H // 2 - 1) as j:
                body(2 * j + 1, 1, j, False, False)
                body(2 * j + 2, 0, j + 1, False, False)
            body(H - 1, 1, H // 2 - 1, False, True)

        def of_head(ap, h, tiles=slice(0, T), cols=slice(0, HE)):
            return ap[:, tiles, bass.ds(h, 1), cols].rearrange("p t o e -> p t (o e)")

        with nc.Block() as block:
            @block.sync
            def _(sp):
                def load(h, b):
                    sp.dma_start(src[:, b, :], src_rows[bass.ds(h, 1), :].to_broadcast([P, N])
                                 ).then_inc(src_loaded[b], 16)
                load(0, 0)
                load(1, 1)
                with sp.Fori(1, H // 2) as hp:
                    for hb in range(2):
                        sp.wait_ge(q_ready, 4 * T * hp + 2 * T * (hb - 1))
                        load(2 * hp + hb, hb)

            @block.vector
            def _(v):
                def choose(h, slot, half, i0, i1):
                    for i in range(i0, i1):
                        if i % QUAD == 0:
                            v.wait_ge(acc_done, G8 * (NQ * (2 * h + half) + i // QUAD + 1))
                        v.scalar_tensor_tensor(out=q[:, i % (2 * QUAD), :],
                                               in0=src[:, slot, half * GW:(half + 1) * GW],
                                               scalar=neg_d[:, i, bass.ds(h, 1)],
                                               in1=mask[:, i, half * GW:(half + 1) * GW],
                                               op0=ALU.is_ge, op1=ALU.mult).then_inc(q_ready, 1)

                def invert(n, b):
                    v.wait_ge(scaled, STEPS * n + STEPS)
                    v.wait_ge(o_free, n + 1)
                    v.reciprocal(rden[:, b, :, :], o[:, b, :, HD:HE]).then_inc(rden_ready, 1)

                def head(h, slot, turn, first, last):
                    v.wait_ge(src_loaded[slot], 16 * turn + 16)
                    choose(h, slot, 0, 0, T - QUAD)
                    if not first:
                        invert(2 * h - 1, 1)
                    choose(h, slot, 0, T - QUAD, T)
                    choose(h, slot, 1, 0, T - QUAD)
                    invert(2 * h, 0)
                    choose(h, slot, 1, T - QUAD, T)

                heads(v, head)
                invert(2 * H - 1, 1)

            @block.scalar
            def _(a):
                a.sem_inc(acc_free, G8)

                def cut_hi(h, slot):
                    for n in range(2):
                        a.wait_ge(whole_ready, 2 * h + n + 1)
                        a.activation(parts[:, slot, :, n * HE:(n + 1) * HE], whole[:], ACT.Copy
                                     ).then_inc(part_hi, 1)

                def take_sums(n, b):
                    a.wait_ge(o_free, n + 1)
                    for t in range(G8):
                        a.wait_ge(acc_done, EARLY + G8 * (NQ * n + NQ - 1) + t + 1)
                        a.activation(o[:, b, t, :], bank[t][:, 0:2 * PW], ACT.Copy).then_inc(acc_free, 1)

                def head(h, slot, turn, first, last):
                    if not last:
                        cut_hi(h + 1, 1 - slot)
                    take_sums(2 * h, 0)
                    take_sums(2 * h + 1, 1)

                cut_hi(0, 0)
                heads(a, head)

            @block.gpsimd
            def _(p):
                p.sem_inc(o_free, 2)
                p.sem_inc(part_lo, 1)

                def cut(h, slot):
                    for n, f in enumerate(("A", "C")):
                        p.wait_ge(part_lo, 2 * h + n + 1)
                        p.tensor_tensor(whole[:], of_head(wh, h),
                                        fac[f][:, :, bass.ds(h, 1)].to_broadcast([P, T, HE]),
                                        ALU.mult).then_inc(whole_ready, 1)
                        p.wait_ge(part_hi, 2 * h + n + 1)
                        p.tensor_tensor(parts[:, slot, :, PW + n * HE:PW + (n + 1) * HE], whole[:],
                                        parts[:, slot, :, n * HE:(n + 1) * HE].bitcast(F32),
                                        ALU.subtract).then_inc(part_lo, 1)

                def combine(h, n, b):
                    tiles = slice(b * G8, (b + 1) * G8)
                    sums = o[:, b, :, 0:PW]
                    a_sum, c_sum = o[:, b, :, 0:HE], o[:, b, :, HE:PW]

                    def step(k, out, in0, in1, op):
                        p.wait_ge(scaled, STEPS * n + k)
                        p.tensor_tensor(out, in0, in1, op).then_inc(scaled, 1)

                    def factor(f):
                        return fac[f][:, tiles, bass.ds(h, 1)].to_broadcast([P, G8, HE])

                    p.wait_ge(acc_free, G8 * (n + 2))
                    p.tensor_tensor(sums, sums, o[:, b, :, PW:2 * PW], ALU.add).then_inc(scaled, 1)
                    step(1, a_sum, a_sum, factor("B"), ALU.mult)
                    step(2, c_sum, c_sum, factor("D"), ALU.mult)
                    step(3, a_sum, a_sum, c_sum, ALU.subtract)
                    step(4, a_sum, a_sum, of_head(md, h, tiles), ALU.add)
                    p.wait_ge(rden_ready, n + 1)
                    p.sem_inc(dividing, 1)
                    p.tensor_tensor(of_head(wh, h, tiles, slice(0, HD)), o[:, b, :, 0:HD],
                                    rden[:, b, :, :].to_broadcast([P, G8, HD]), ALU.mult).then_inc(o_free, 1)

                def head(h, slot, turn, first, last):
                    if not last:
                        cut(h + 1, 1 - slot)
                    combine(h, 2 * h, 0)
                    combine(h, 2 * h + 1, 1)

                cut(0, 0)
                heads(p, head)

            @block.tensor
            def _(pe):
                pe.sem_inc(acc_done, EARLY)
                with pe.Fori(0, H // 2) as hp:
                    for slot in range(2):
                        h = 2 * hp + slot
                        for half in range(2):
                            n = 2 * h + half
                            for quad in range(NQ):
                                pe.wait_ge(part_lo, 2 * h + 3)
                                pe.wait_ge(q_ready, T * n + QUAD * quad + QUAD)
                                for t in range(G8):
                                    if quad == 0:
                                        pe.wait_ge(acc_free, G8 * n + t + 1)
                                    for b in range(QUAD):
                                        i = QUAD * quad + b
                                        mm = pe.matmul(bank[t][:, 0:2 * PW],
                                                       q[:, i % (2 * QUAD), t * P:(t + 1) * P],
                                                       parts[:, slot, i, :], start=i == 0, stop=i == T - 1,
                                                       skip_group_check=True)
                                    mm.then_inc(acc_done, 1)


def feed_forward(nc, bank, wh, ident, x1_store, w1_t, b1, w2_t, b2, w3_t, b3, w4_t, b4, out):
    F1, F2, F3 = w1_t.shape[1], w2_t.shape[1], w3_t.shape[1]
    K1, K3 = F1 // P, F3 // P
    TC = 4
    CW = TC * P
    with ExitStack() as ctx:
        def sb(name, shape, dt=F32):
            return ctx.enter_context(nc.sbuf_tensor(name, shape, dt))

        def sem(name):
            return ctx.enter_context(nc.semaphore(name))

        w1_s = sb("l5_w1", [P, KC, F1])
        w2_s = sb("l5_w2", [P, K1, F2])
        w3_s = sb("l5_w3", [P, F3])
        w4_s = sb("l5_w4", [P, K3, F])
        b1_s = sb("l5_b1", [P, K1])
        b2_s = sb("l5_b2", [P, 1])
        b3_s = sb("l5_b3", [P, K3])
        b4_s = sb("l5_b4", [P, 1, F])
        neg = sb("l5_neg", [P, TC * H, HD])
        enc = sb("l5_enc", [P, TC, F])
        enc_t = sb("l5_enc_t", [P, KC, CW])
        o1 = sb("l5_o1", [P, K1, CW])
        o2 = sb("l5_o2", [P, CW])
        o3 = sb("l5_o3", [P, K3, CW])
        res = sb("l5_res", [P, TC, F])

        w_loaded = sem("l5_w_loaded")
        x_loaded = sem("l5_x_loaded")
        neg_ready = sem("l5_neg_ready")
        exp_ready = sem("l5_exp_ready")
        pos_ready = sem("l5_pos_ready")
        enc_ready = sem("l5_enc_ready")
        turned = sem("l5_turned")
        enc_t_ready = sem("l5_enc_t_ready")
        sums_done = sem("l5_sums_done")
        act_ready = sem("l5_act_ready")
        biased = sem("l5_biased")
        rows_done = sem("l5_rows_done")
        out_ready = sem("l5_out_ready")
        stored = sem("l5_stored")
        zs = wh[:].rearrange("p t h e -> p (t h) e")

        with nc.Block() as block:
            @block.sync
            def _(sp):
                for dst, src in ((w1_s, w1_t.rearrange("(k p) f -> p k f", p=P)),
                                 (w2_s, w2_t.rearrange("(k p) f -> p k f", p=P)),
                                 (w3_s, w3_t), (w4_s, w4_t.rearrange("(k p) f -> p k f", p=P)),
                                 (b1_s, b1), (b2_s, b2), (b3_s, b3)):
                    sp.dma_start(dst[:], src).then_inc(w_loaded, 16)
                sp.dma_start(b4_s[:, 0, :], b4.rearrange("(o f) -> o f", o=1).to_broadcast([P, F])
                             ).then_inc(w_loaded, 16)
                sp.sem_inc(stored, 16)
                with sp.Fori(0, T // TC) as c:
                    rows = bass.ds(c * CW, CW)
                    sp.wait_ge(stored, 16 * c + 16)
                    sp.dma_start(res[:], x1_store[rows, :].rearrange("(t p) f -> p t f", p=P)
                                 ).then_inc(x_loaded, 16)
                    sp.wait_ge(out_ready, TC * c + 2 * TC)
                    sp.dma_start(out[rows, :].rearrange("(t p) f -> p t f", p=P), res[:]).then_inc(stored, 16)
                sp.wait_ge(stored, 16 * (T // TC + 1))

            @block.vector
            def _(v):
                v.sem_inc(enc_ready, 1)
                v.sem_inc(out_ready, TC)
                v.wait_ge(w_loaded, 16 * 8)
                with v.Fori(0, T // TC) as c:
                    z = zs[:, bass.ds(c * TC * H, TC * H), 0:HD]
                    v.wait_ge(enc_ready, c + 1)
                    v.tensor_scalar(neg[:], z, 0.0, None, ALU.min).then_inc(neg_ready, 1)
                    v.wait_ge(turned, KC * c + KC)
                    enc_z = enc[:].rearrange("p t (h d) -> p (t h) d", h=H)
                    v.tensor_scalar(enc_z, z, 0.0, -1.0, ALU.max, ALU.add).then_inc(pos_ready, 1)
                    v.wait_ge(exp_ready, c + 1)
                    v.wait_ge(pos_ready, c + 1)
                    v.tensor_tensor(enc_z, enc_z, neg[:], ALU.add).then_inc(enc_ready, 1)
                    for k in range(KC):
                        v.wait_ge(turned, KC * c + KC + k + 1)
                        v.tensor_copy(enc_t[:, k, :], bank[k][:]).then_inc(enc_t_ready, 1)
                    v.wait_ge(x_loaded, 16 * c + 16)
                    v.tensor_tensor(res[:], res[:], b4_s[:].to_broadcast([P, TC, F]), ALU.add).then_inc(biased, 1)
                    v.wait_ge(biased, c + 1)
                    for t in range(TC):
                        v.wait_ge(rows_done, TC * c + t + 1)
                        v.tensor_tensor(res[:, t, :], bank[t][:], res[:, t, :], ALU.add).then_inc(out_ready, 1)

            @block.scalar
            def _(a):
                a.wait_ge(w_loaded, 16 * 8)
                with a.Fori(0, T // TC) as c:
                    a.wait_ge(neg_ready, c + 1)
                    a.activation(neg[:], neg[:], ACT.Exp).then_inc(exp_ready, 1)
                    a.wait_ge(sums_done, 5 * c + 2)
                    for k in range(K1):
                        a.activation(o1[:, k, :], bank[4 + k][:], ACT.Relu, bias=b1_s[:, k:k + 1]
                                     ).then_inc(act_ready, 1)
                    a.wait_ge(sums_done, 5 * c + 3)
                    a.activation(o2[:], bank[6][:], ACT.Relu, bias=b2_s[:, 0:1]).then_inc(act_ready, 1)
                    a.wait_ge(sums_done, 5 * c + 5)
                    for k in range(K3):
                        a.activation(o3[:, k, :], bank[4 + k][:], ACT.Relu, bias=b3_s[:, k:k + 1]
                                     ).then_inc(act_ready, 1)

            @block.tensor
            def _(pe):
                pe.sem_inc(turned, KC)
                pe.wait_ge(w_loaded, 16 * 8)
                with pe.Fori(0, T // TC) as c:
                    pe.wait_ge(enc_ready, c + 2)
                    for k in range(KC):
                        pe.wait_ge(out_ready, TC * c + k + 1)
                        for t in range(TC):
                            mm = pe.transpose(bank[k][:, t * P:(t + 1) * P], enc[:, t, k * P:(k + 1) * P], ident[:])
                        mm.then_inc(turned, 1)
                    pe.wait_ge(enc_t_ready, KC * c + KC)
                    for m in range(K1):
                        for k in range(KC):
                            mm = pe.matmul(bank[4 + m][:], w1_s[:, k, m * P:(m + 1) * P], enc_t[:, k, :],
                                           start=k == 0, stop=k == KC - 1)
                        mm.then_inc(sums_done, 1)
                    pe.wait_ge(act_ready, 5 * c + 2)
                    for k in range(K1):
                        mm = pe.matmul(bank[6][:], w2_s[:, k, :], o1[:, k, :], start=k == 0, stop=k == K1 - 1)
                    mm.then_inc(sums_done, 1)
                    pe.wait_ge(act_ready, 5 * c + 3)
                    for m in range(K3):
                        pe.matmul(bank[4 + m][:], w3_s[:, m * P:(m + 1) * P], o2[:], start=True, stop=True
                                  ).then_inc(sums_done, 1)
                    pe.wait_ge(act_ready, 5 * c + 5)
                    for t in range(TC):
                        for k in range(K3):
                            mm = pe.matmul(bank[t][:], o3[:, k, t * P:(t + 1) * P], w4_s[:, k, :],
                                           start=k == 0, stop=k == K3 - 1)
                        mm.then_inc(rows_done, 1)


def build(nc, x, adj, adj_t, w, a1, a2, w1_t, b1, w2_t, b2, w3_t, b3, w4_t, b4, out):
    src_rows = nc.dram_tensor("src_rows", (H, N), F32, kind="Internal").ap()
    dst_top = nc.dram_tensor("dst_top", (H, 1), F32, kind="Internal").ap()
    x1_store = nc.dram_tensor("x1_store", (N, F), F32, kind="Internal").ap()
    with ExitStack() as ctx:
        def sb(name, shape, dt=F32, within=ctx):
            return within.enter_context(nc.sbuf_tensor(name, shape, dt))

        bank = [ctx.enter_context(nc.psum_tensor(f"bank{k}", [P, 512], F32)) for k in range(8)]
        ident = sb("ident", [P, P])
        make_identity(nc, ident)
        rstd = sb("rstd", [P, T])
        nmr = sb("nmr", [P, T])
        e = sb("e", [P, T, 2 * H])
        smooth = ctx.enter_context(ExitStack())
        G = smooth.enter_context(nc.sbuf_tensor("G", [P, T, F], F32, side="right"))
        smooth_features(nc, bank, G, x, adj, adj_t)
        mask = sb("mask", [P, T, N], U8)
        wh = sb("wh", [P, T, H, HE])
        with nc.sbuf_tensor("x1", [P, T, F], F32) as x1:
            spread_features(nc, bank, G, x1, mask, rstd, nmr, x, adj_t)
            smooth.close()
            project_heads(nc, bank, x1, rstd, nmr, wh, e, ident, w, a1, a2, src_rows, dst_top, x1_store)
        fac = {f: sb(f"fac_{f}", [P, T, H]) for f in "ABCD"}
        neg_d = sb("neg_d", [P, T, H])
        md = sb("md", [P, T, H, HE])
        edge_factors(nc, bank, wh, e, mask, fac, neg_d, md, dst_top)
        attend(nc, bank, wh, mask, fac, neg_d, md, src_rows)
        feed_forward(nc, bank, wh, ident, x1_store, w1_t, b1, w2_t, b2, w3_t, b3, w4_t, b4, out)


_WEIGHTS = ("a1", "a2", "W1", "b1", "W2", "b2", "W3", "b3", "W4", "b4")


def kernel(x, adj, L1_gnn_W, **weights):
    import numpy as np
    import concourse.bacc as bacc
    from concourse.bass_utils import run_bass_kernel_spmd

    nc = bacc.Bacc("TRN2", target_bir_lowering=False, num_devices=1)
    arrays = {"x": x, "adj": adj, "adj_t": np.asarray(adj).T, "w": L1_gnn_W}
    for name in _WEIGHTS:
        a = np.asarray(weights[f"L1_gnn_{name}"])
        if name in ("b1", "b2", "b3"):
            a = a.reshape(-1, P)
        arrays[name] = a.T if a.ndim == 2 and name[0] != "a" else a
    arrays = {name: np.ascontiguousarray(a) for name, a in arrays.items()}
    aps = [nc.dram_tensor(name, a.shape, mybir.dt.from_np(a.dtype), kind="ExternalInput").ap()
           for name, a in arrays.items()]
    out = nc.dram_tensor("out", (N, F), F32, kind="ExternalOutput").ap()
    build(nc, *aps, out)
    return run_bass_kernel_spmd(nc, [arrays], core_ids=[0]).results[0]["out"]
```

```python
from contextlib import ExitStack, nullcontext

import concourse.bass as bass
from concourse import mybir

F32 = mybir.dt.float32
F32R = mybir.dt.float32r
U8 = mybir.dt.uint8
ALU = mybir.AluOpType
ACT = mybir.ActivationFunctionType
AX_X = mybir.AxisListType.X

P = 128
N = 2048
F = 512
T = N // P
H = 8
HD = F // H
HE = HD + 1
KC = F // P
G8 = 8
GW = G8 * P
SLOTS = 4
LNT = 4
NLN = T // LNT
EPS = 1e-5
SLOPE = 0.2
LEAST_SUM = 1e-20
TINY = 1e-30


def refine_rsqrt(v, chain, count, d, root, y, tmp):
    v.reciprocal(y, root).then_inc(chain, 1)
    v.wait_ge(chain, count + 1)
    v.tensor_tensor(tmp, y, y, ALU.mult).then_inc(chain, 1)
    v.wait_ge(chain, count + 2)
    v.tensor_tensor(tmp, tmp, d, ALU.mult).then_inc(chain, 1)
    v.wait_ge(chain, count + 3)
    v.tensor_scalar(tmp, tmp, -0.5, 1.5, ALU.mult, ALU.add).then_inc(chain, 1)
    v.wait_ge(chain, count + 4)
    v.tensor_tensor(y, y, tmp, ALU.mult).then_inc(chain, 1)
    v.wait_ge(chain, count + 5)


def split_product(pe, acc, hi, lo, rhs_hi, rhs_lo, first):
    pe.matmul(acc, hi, rhs_hi, start=first, stop=False, skip_group_check=True)
    pe.matmul(acc, hi, rhs_lo, start=False, stop=False, skip_group_check=True)
    return pe.matmul(acc, lo, rhs_hi, start=False, stop=True, skip_group_check=True)


def skewed(eng, count, stages, pause=None):
    most = max(stage[1] for stage in stages)

    def turn(k, parity, first, last):
        for work, lag, *tiles in stages:
            if first >= lag and last - lag < (tiles[0] if tiles else count):
                work(k - lag, (parity + lag) % 2)

    def turns(first, end):
        pairs = (end - first) // 2
        with eng.Fori(0, pairs) as j:
            for b in range(2):
                turn(2 * j + first + b, (first + b) % 2, first, end - 1)
        if (end - first) % 2:
            turn(end - 1, (end - 1) % 2, end - 1, end - 1)

    for k in range(most):
        turn(k, k % 2, k, k)
    if pause:
        turns(most, pause[0])
        pause[1]()
        turns(pause[0], count)
    elif most < count:
        turns(most, count)
    for k in range(count, count + most):
        turn(k, k % 2, k, k)


def if_set(eng, flag):
    if flag is None:
        return nullcontext()
    return eng.If(eng.value_load(flag[0:1, 0:1], min_val=0, max_val=1) > 0)


def make_identity(nc, ident):
    with nc.semaphore("ident_zeroed") as zeroed, nc.Block() as block:
        @block.gpsimd
        def _(g):
            g.memset(ident[:], 0.0).then_inc(zeroed, 1)
            g.wait_ge(zeroed, 1)
            g.affine_select(out=ident[:], in_=ident[:], compare_op=ALU.not_equal, fill=1.0, base=0,
                            pattern=[[-1, P]], channel_multiplier=1)


def load_half_rows(sp, rows, rows_loaded, adj_t, half, i, slot):
    sp.dma_start(rows[:, slot, :], adj_t[bass.ds(i * P, P), half * GW:(half + 1) * GW]
                 ).then_inc(rows_loaded[slot], 16)


def smooth_features(nc, bank, G, rows, rows_loaded, x, adj, adj_t):
    with ExitStack() as ctx:
        def sb(name, shape, dt=F32):
            return ctx.enter_context(nc.sbuf_tensor(name, shape, dt))

        def sem(name):
            return ctx.enter_context(nc.semaphore(name))

        h = sb("l0_h", [P, T, F])
        sum_a = sb("l0_sum_a", [P, SLOTS, GW])
        sum_b = sb("l0_sum_b", [P, T, GW])
        rows_b = sb("l0_rows_b", [P, SLOTS, GW])
        s_hi = sb("l0_s_hi", [P, 2, GW], F32R)
        s_lo = sb("l0_s_lo", [P, 2, GW], F32R)
        x_hi = sb("l0_x_hi", [P, 2, F], F32R)
        x_lo = sb("l0_x_lo", [P, 2, F], F32R)
        stats = sb("l0_stats", [P, T, 6])
        mv = sb("l0_mv", [P, T, 2])
        var = sb("l0_var", [P, T])
        root = sb("l0_root", [P, T])
        rstd = sb("l0_rstd", [P, T])
        nmr = sb("l0_nmr", [P, T])
        tmp = sb("l0_tmp", [P, T])
        part = sb("l0_part", [P, T, 2])
        deg = sb("l0_deg", [P, T, 1])
        pos = sb("l0_pos", [P, T, 1])
        degc = sb("l0_degc", [P, T, 1])
        droot = sb("l0_droot", [P, T, 1])
        y = sb("l0_y", [P, T, 1])
        ytmp = sb("l0_ytmp", [P, T, 1])
        dinv = sb("l0_dinv", [P, T, 1])
        hdinv = sb("l0_hdinv", [P, T, 1])

        x_loaded = [sem(f"l0_x_loaded{c}") for c in range(NLN)]
        sums_loaded = [sem(f"l0_sums_loaded{b}") for b in range(SLOTS)]
        ln_chain = sem("l0_ln_chain")
        var_ready = sem("l0_var_ready")
        ln_root = sem("l0_ln_root")
        norm_ready = sem("l0_norm_ready")
        h_ready = sem("l0_h_ready")
        summed = sem("l0_summed")
        deg_chain = sem("l0_deg_chain")
        pos_ready = sem("l0_pos_ready")
        inv_chain = sem("l0_inv_chain")
        deg_ready = sem("l0_deg_ready")
        root_ready = sem("l0_root_ready")
        hi_ready = sem("l0_hi_ready")
        lo_ready = sem("l0_lo_ready")
        x_chain = sem("l0_x_chain")
        x_ready = sem("l0_x_ready")
        slot_free = sem("l0_slot_free")
        acc_done = sem("l0_acc_done")
        base_ready = sem("l0_base_ready")
        g_done = sem("l0_g_done")
        INV = 5

        with nc.Block() as block:
            @block.sync
            def _(sp):
                def load(i, b):
                    tile = bass.ds(i * P, P)
                    load_half_rows(sp, rows, rows_loaded, adj_t, 0, i, b)
                    sp.dma_start(sum_a[:, b, :], adj[tile, 0:GW]).then_inc(sums_loaded[b], 16)
                    sp.dma_start(rows_b[:, b, :], adj_t[tile, GW:N]).then_inc(sums_loaded[b], 16)
                    sp.dma_start(sum_b[:, i, :], adj[tile, GW:N]).then_inc(sums_loaded[b], 16)

                for b in range(SLOTS):
                    if b < NLN:
                        sp.dma_start(h[:, b * LNT:(b + 1) * LNT, :], x[b * LNT * P:(b + 1) * LNT * P, :].rearrange(
                            "(t p) f -> p t f", p=P)).then_inc(x_loaded[b], 16)
                    load(b, b)
                with sp.Fori(1, T // SLOTS) as j:
                    for b in range(SLOTS):
                        sp.wait_ge(deg_ready, SLOTS * j + b + 1 - SLOTS)
                        sp.wait_ge(lo_ready, SLOTS * j + b + 1 - SLOTS)
                        load(SLOTS * j + b, b)
                sp.wait_ge(summed, 2 * T)
                for b in range(SLOTS):
                    load_half_rows(sp, rows, rows_loaded, adj_t, 0, b, b)

            @block.vector
            def _(v):
                def norms(c):
                    part_of = slice(c * LNT, (c + 1) * LNT)
                    base = (2 * LNT + 5) * c
                    v.wait_ge(x_loaded[c], 16)
                    for t in range(c * LNT, (c + 1) * LNT):
                        v.bn_stats(stats[:, t, :], h[:, t, :]).then_inc(ln_chain, 1)
                    for k in range(LNT):
                        t = c * LNT + k
                        v.wait_ge(ln_chain, base + k + 1)
                        v.bn_aggr(mv[:, t, :], stats[:, t, :]).then_inc(ln_chain, 1)
                    v.wait_ge(ln_chain, base + 2 * LNT)
                    v.tensor_scalar(var[:, part_of], mv[:, part_of, 1], EPS, None, ALU.add).then_inc(var_ready, 1)
                    v.wait_ge(ln_root, c + 1)
                    refine_rsqrt(v, ln_chain, base + 2 * LNT, var[:, part_of], root[:, part_of],
                                 rstd[:, part_of], tmp[:, part_of])
                    v.scalar_tensor_tensor(out=nmr[:, part_of], in0=mv[:, part_of, 0], scalar=-1.0,
                                           in1=rstd[:, part_of], op0=ALU.mult, op1=ALU.mult
                                           ).then_inc(norm_ready, 1)

                def x_parts(i, b, s):
                    v.wait_ge(slot_free, s + 1)
                    v.tensor_scalar(x_hi[:, b, :], h[:, i, :], dinv[:, i, :], None,
                                    ALU.mult).then_inc(x_chain, 1)
                    v.wait_ge(x_chain, s + 1)
                    v.scalar_tensor_tensor(out=x_lo[:, b, :], in0=h[:, i, :], scalar=dinv[:, i, :],
                                           in1=x_hi[:, b, :].bitcast(F32), op0=ALU.mult,
                                           op1=ALU.subtract).then_inc(x_ready, 1)

                def add_rows(turn, slot):
                    i = SLOTS * turn + slot

                    def half_a():
                        v.wait_ge(rows_loaded[slot], 16 * turn + 16)
                        v.wait_ge(sums_loaded[slot], 48 * turn + 48)
                        v.scalar_tensor_tensor(out=sum_a[:, slot, :], in0=rows[:, slot, :], scalar=1.0,
                                               in1=sum_a[:, slot, :], op0=ALU.mult, op1=ALU.add,
                                               accum_out=part[:, i, 0:1]).then_inc(summed, 1)

                    def half_b():
                        v.scalar_tensor_tensor(out=sum_b[:, i, :], in0=rows_b[:, slot, :], scalar=1.0,
                                               in1=sum_b[:, i, :], op0=ALU.mult, op1=ALU.add,
                                               accum_out=part[:, i, 1:2]).then_inc(summed, 1)

                    def degree():
                        v.wait_ge(summed, 2 * i + 2)
                        v.tensor_scalar(deg[:, i, :], part[:, i, 0:1], part[:, i, 1:2], 2.0, ALU.add,
                                        ALU.add).then_inc(deg_chain, 1)

                    def guard():
                        v.wait_ge(deg_chain, i + 1)
                        v.tensor_scalar(degc[:, i, :], deg[:, i, :], TINY, None, ALU.max).then_inc(deg_ready, 1)
                        v.tensor_scalar(pos[:, i, :], deg[:, i, :], 0.0, None, ALU.is_gt).then_inc(pos_ready, 1)

                    return half_a, half_b, degree, guard

                def invert(i, b):
                    c = INV * i

                    def first():
                        v.wait_ge(root_ready, i + 1)
                        v.reciprocal(y[:, i, :], droot[:, i, :]).then_inc(inv_chain, 1)

                    def square():
                        v.wait_ge(inv_chain, c + 1)
                        v.scalar_tensor_tensor(out=ytmp[:, i, :], in0=y[:, i, :], scalar=degc[:, i, :],
                                               in1=y[:, i, :], op0=ALU.mult, op1=ALU.mult).then_inc(inv_chain, 1)

                    def correct():
                        v.wait_ge(inv_chain, c + 2)
                        v.tensor_scalar(ytmp[:, i, :], ytmp[:, i, :], -0.25, 1.5, ALU.mult,
                                        ALU.add).then_inc(inv_chain, 1)

                    def last():
                        v.wait_ge(inv_chain, c + 3)
                        v.wait_ge(pos_ready, i + 1)
                        v.scalar_tensor_tensor(out=dinv[:, i, :], in0=ytmp[:, i, :], scalar=y[:, i, :],
                                               in1=pos[:, i, :], op0=ALU.mult, op1=ALU.mult
                                               ).then_inc(inv_chain, 1)

                    def product():
                        v.wait_ge(inv_chain, c + 4)
                        v.wait_ge(h_ready, i + 1)
                        v.tensor_scalar(hdinv[:, i, :], dinv[:, i, :], 0.5, None, ALU.mult).then_inc(inv_chain, 1)
                        x_parts(i, b, i)

                    return first, square, correct, last, product

                def step(turn, slot, before):
                    half_a, half_b, degree, guard = add_rows(turn, slot)
                    if before:
                        first, square, correct, last, product = invert(SLOTS * turn + slot - 1, (slot + 1) % 2)
                    half_a()
                    if before:
                        first()
                    half_b()
                    if before:
                        square()
                    degree()
                    if before:
                        correct()
                    guard()
                    if before:
                        last()
                        product()

                norms(0)
                step(0, 0, False)
                for link in invert(0, 0):
                    link()
                for slot in range(1, SLOTS):
                    if slot < NLN:
                        norms(slot)
                    step(0, slot, slot > 1)
                with v.Fori(1, T // SLOTS) as j:
                    for slot in range(SLOTS):
                        step(j, slot, True)
                for link in invert(T - 1, 1):
                    link()
                v.wait_ge(inv_chain, INV * T)

                def write_base(g):
                    for n in range(G8 * g, G8 * (g + 1)):
                        v.tensor_scalar(G[:, n, :], h[:, n, :], dinv[:, n, :], dinv[:, n, :],
                                        ALU.mult, ALU.mult).then_inc(base_ready, 1)

                def write_g(g):
                    for k in range(G8):
                        n = G8 * g + k
                        v.wait_ge(base_ready, n + 1)
                        v.wait_ge(acc_done, n + 1)
                        v.scalar_tensor_tensor(out=G[:, n, :], in0=bank[k][:], scalar=hdinv[:, n, :],
                                               in1=G[:, n, :], op0=ALU.mult, op1=ALU.add).then_inc(g_done, 1)

                write_base(0)
                x_parts(0, 0, T)
                write_g(0)
                x_parts(1, 1, T + 1)
                with v.Fori(1, T // 2) as j:
                    for b in range(2):
                        x_parts(2 * j + b, b, T + 2 * j + b)
                write_base(1)
                write_g(1)

            @block.scalar
            def _(a):
                def normalise(c):
                    part_of = slice(c * LNT, (c + 1) * LNT)
                    a.wait_ge(var_ready, c + 1)
                    a.activation(root[:, part_of], var[:, part_of], ACT.Sqrt).then_inc(ln_root, 1)
                    a.wait_ge(norm_ready, c + 1)
                    for t in range(c * LNT, (c + 1) * LNT):
                        a.activation(h[:, t, :], h[:, t, :], ACT.Relu, bias=nmr[:, t:t + 1],
                                     scale=rstd[:, t:t + 1]).then_inc(h_ready, 1)

                def cut_first(turn, slot):
                    i = SLOTS * turn + slot
                    a.wait_ge(deg_ready, i + 1)
                    a.activation(droot[:, i, :], degc[:, i, :], ACT.Sqrt, scale=0.5).then_inc(root_ready, 1)
                    a.wait_ge(slot_free, i + 1)
                    a.activation(s_hi[:, slot % 2, :], sum_a[:, slot, :], ACT.Copy).then_inc(hi_ready, 1)

                for slot in range(SLOTS):
                    if slot < NLN:
                        normalise(slot)
                    cut_first(0, slot)
                with a.Fori(1, T // SLOTS) as j:
                    for slot in range(SLOTS):
                        cut_first(j, slot)
                with a.Fori(0, T // 2) as j:
                    for b in range(2):
                        i = 2 * j + b
                        a.wait_ge(slot_free, T + i + 1)
                        a.activation(s_hi[:, b, :], sum_b[:, i, :], ACT.Copy).then_inc(hi_ready, 1)

            @block.gpsimd
            def _(g):
                with g.Fori(0, T // SLOTS) as j:
                    for slot in range(SLOTS):
                        g.wait_ge(hi_ready, SLOTS * j + slot + 1)
                        g.tensor_tensor(s_lo[:, slot % 2, :], sum_a[:, slot, :], s_hi[:, slot % 2, :].bitcast(F32),
                                        ALU.subtract).then_inc(lo_ready, 1)
                with g.Fori(0, T // 2) as j:
                    for b in range(2):
                        g.wait_ge(hi_ready, T + 2 * j + b + 1)
                        g.tensor_tensor(s_lo[:, b, :], sum_b[:, 2 * j + b, :], s_hi[:, b, :].bitcast(F32),
                                        ALU.subtract).then_inc(lo_ready, 1)

            @block.tensor
            def _(pe):
                pe.sem_inc(slot_free, 2)

                def products(s, b, g, first, last):
                    pe.wait_ge(lo_ready, s + 1)
                    pe.wait_ge(x_ready, s + 1)
                    for k in range(G8):
                        if first and g == 1:
                            pe.wait_ge(g_done, k + 1)
                        cols = slice(k * P, (k + 1) * P)
                        mm = split_product(pe, bank[k][:], s_hi[:, b, cols], s_lo[:, b, cols],
                                           x_hi[:, b, :], x_lo[:, b, :], first)
                        if last:
                            mm.then_inc(acc_done, 1)
                    if not last:
                        mm.then_inc(slot_free, 1)

                for g in range(2):
                    products(T * g, 0, g, True, False)
                    with pe.Fori(0, T // 2 - 1) as j:
                        products(T * g + 2 * j + 1, 1, g, False, False)
                        products(T * g + 2 * j + 2, 0, g, False, False)
                    products(T * g + T - 1, 1, g, False, True)
                    if g == 0:
                        pe.wait_ge(acc_done, G8)
                        pe.sem_inc(slot_free, 1)


def spread_and_project(nc, bank, G, rows, rows_loaded, x1, mask, wh, e, ident, x, adj_t, w, a1, a2, e_rows,
                       dst_top, x1_store):
    with ExitStack() as ctx:
        def sb(name, shape, dt=F32):
            return ctx.enter_context(nc.sbuf_tensor(name, shape, dt))

        def sem(name):
            return ctx.enter_context(nc.semaphore(name))

        a_hi = sb("l1_a_hi", [P, 2, GW], F32R)
        a_lo = sb("l1_a_lo", [P, 2, GW], F32R)
        g_hi = sb("l1_g_hi", [P, 2, F], F32R)
        g_lo = sb("l1_g_lo", [P, 2, F], F32R)
        stats = sb("l1_stats", [P, T, 6])
        mv = sb("l1_mv", [P, T, 2])
        var = sb("l1_var", [P, T])
        root = sb("l1_root", [P, T])
        tmp = sb("l1_tmp", [P, T])
        rstd = sb("l1_rstd", [P, T])
        nmr = sb("l1_nmr", [P, T])

        x_loaded = sem("l1_x_loaded")
        hi_ready = sem("l1_hi_ready")
        lo_ready = sem("l1_lo_ready")
        g_chain = sem("l1_g_chain")
        g_ready = sem("l1_g_ready")
        mask_done = sem("l1_mask_done")
        slot_free = sem("l1_slot_free")
        acc_done = sem("l1_acc_done")
        x1_done = sem("l1_x1_done")
        stats_done = sem("l1_stats_done")
        mv_done = sem("l1_mv_done")
        var_ready = sem("l1_var_ready")
        ln_root = sem("l1_ln_root")
        ln_chain = sem("l1_ln_chain")
        norm_ready = sem("l1_norm_ready")

        w_f = sb("l2_w", [P, KC, H, HD])
        w_hi = sb("l2_w_hi", [P, KC, F], F32R)
        w_lo = sb("l2_w_lo", [P, KC, F], F32R)
        a_b = sb("l2_a", [P, 2, F])
        e_t = rows[0:2 * H, 0:2, :].rearrange("p b n -> p (b n)")
        h2 = rows[:, 2, :].rearrange("p (b f) -> p b f", b=2)
        prod = sb("l2_prod", [P, 2, 2, F])
        top = sb("l2_top", [2 * H, 1])
        tops = sb("l2_tops", [2 * H, 4])
        top_w = sb("l2_top_w", [2 * H, P])

        w_loaded = sem("l2_w_loaded")
        w_chain = sem("l2_w_chain")
        w_ready = sem("l2_w_ready")
        h_ready = sem("l2_h_ready")
        turned = sem("l2_turned")
        t_hi_ready = sem("l2_t_hi_ready")
        t_lo_ready = sem("l2_t_lo_ready")
        wh_summed = sem("l2_wh_summed")
        wh_ready = sem("l2_wh_ready")
        table_loaded = sem("l2_table_loaded")
        prod_ready = sem("l2_prod_ready")
        e_ready = sem("l2_e_ready")
        e_turned = sem("l2_e_turned")
        e_copied = sem("l2_e_copied")
        top_ready = sem("l2_top_ready")
        stored = sem("l2_stored")
        top_spread = sem("l2_top_spread")
        x1_stored = sem("l2_x1_stored")

        def per_head(ap):
            return ap.rearrange("p (h d) -> p h d", h=H)

        with nc.Block() as block:
            @block.sync
            def _(sp):
                sp.dma_start(x1[:], x.rearrange("(t p) f -> p t f", p=P)).then_inc(x_loaded, 16)
                for k in range(KC):
                    sp.dma_start(w_f[:, k, :, :], w[:, k * P:(k + 1) * P, :].rearrange("h p d -> p h d")
                                 ).then_inc(w_loaded, 16)
                for n, a in enumerate((a1, a2)):
                    row = a.rearrange("h d -> (h d)").rearrange("(o f) -> o f", o=1)
                    sp.dma_start(a_b[:, n, :], row.to_broadcast([P, F])).then_inc(w_loaded, 16)
                for g in range(2):
                    with sp.Fori(1 - g, T // SLOTS) as j:
                        for r in range(SLOTS):
                            sp.wait_ge(lo_ready, T * g + SLOTS * j + r + 1 - SLOTS)
                            sp.wait_ge(mask_done, T * g + SLOTS * j + r + 1 - SLOTS)
                            load_half_rows(sp, rows, rows_loaded, adj_t, g, SLOTS * j + r, r)
                sp.wait_ge(x1_done, T)
                sp.dma_start(x1_store.rearrange("(t p) f -> p t f", p=P), x1[:]).then_inc(x1_stored, 16)
                sp.wait_ge(e_copied, 4)
                sp.dma_start(e_rows, e_t).then_inc(stored, 16)
                sp.wait_ge(stored, 16)
                sp.wait_ge(x1_stored, 16)

            @block.scalar
            def _(a):
                def cut_hi(g, turns):
                    with a.Fori(*turns) as j:
                        for r in range(SLOTS):
                            a.wait_ge(rows_loaded[r], 16 * (T // SLOTS * (1 + g) + j) + 16)
                            a.wait_ge(slot_free, T * g + SLOTS * j + r + 1)
                            a.activation(a_hi[:, r % 2, :], rows[:, r, :], ACT.Copy).then_inc(hi_ready, 1)

                def roots(g):
                    half = slice(G8 * g, G8 * (g + 1))
                    a.wait_ge(var_ready, g + 1)
                    a.activation(root[:, half], var[:, half], ACT.Sqrt).then_inc(ln_root, 1)

                cut_hi(0, (0, T // SLOTS))
                cut_hi(1, (0, 3))
                roots(0)
                cut_hi(1, (3, T // SLOTS))

                def cut_turned(t, b):
                    a.wait_ge(turned, t + 3)
                    a.wait_ge(wh_summed, t + 1)
                    a.activation(g_hi[:, b, :], bank[b][:], ACT.Copy).then_inc(t_hi_ready, 1)

                def normalise(t, b):
                    a.wait_ge(turned, t + 1)
                    a.activation(h2[:, b, :], x1[:, t, :], ACT.Relu, bias=nmr[:, bass.ds(t, 1)],
                                 scale=rstd[:, bass.ds(t, 1)]).then_inc(h_ready, 1)

                def take_wh(t, b):
                    a.wait_ge(wh_summed, t + 3)
                    a.activation(wh[:, t, :, 0:HD], per_head(bank[2 + b][:]), ACT.Copy).then_inc(wh_ready, 1)

                a.sem_inc(wh_ready, 2)
                def second_roots():
                    roots(1)
                    a.wait_ge(norm_ready, 2)

                a.wait_ge(norm_ready, 1)
                a.wait_ge(mask_done, 2 * T)
                skewed(a, T, ((normalise, 0), (cut_turned, 1), (take_wh, 2)), (5, second_roots))
                a.activation(root[:], root[:], ACT.Exp, scale=0.0).then_inc(table_loaded, 1)

            @block.gpsimd
            def _(p):
                p.sem_inc(prod_ready, 1)

                def products(t, b):
                    p.wait_ge(wh_ready, t + 3)
                    p.wait_ge(e_ready, 2 * t + 2)
                    for n in range(2):
                        p.tensor_tensor(per_head(prod[:, b, n, :]), wh[:, t, :, 0:HD], per_head(a_b[:, n, :]),
                                        ALU.mult).then_inc(prod_ready, 1)
                skewed(p, T, ((products, 0),))

            @block.vector
            def _(v):
                v.memset(wh[:, :, :, HD:HE], 1.0)

                def cut(g, j, r):
                    i, s, b = SLOTS * j + r, T * g + SLOTS * j + r, r % 2
                    v.wait_ge(slot_free, s + 1)
                    v.tensor_copy(g_hi[:, b, :], G[:, i, :]).then_inc(g_chain, 1)
                    v.wait_ge(g_chain, s + 1)
                    v.tensor_tensor(g_lo[:, b, :], G[:, i, :], g_hi[:, b, :].bitcast(F32),
                                    ALU.subtract).then_inc(g_ready, 1)
                    v.wait_ge(hi_ready, s + 1)
                    v.tensor_tensor(a_lo[:, b, :], rows[:, r, :], a_hi[:, b, :].bitcast(F32),
                                    ALU.subtract).then_inc(lo_ready, 1)
                    v.tensor_scalar(mask[:, i, g * GW:(g + 1) * GW], rows[:, r, :], 0.0, None,
                                    ALU.is_gt).then_inc(mask_done, 1)

                def add_y(g):
                    for k in range(G8):
                        n = G8 * g + k
                        v.wait_ge(acc_done, n + 1)
                        v.tensor_tensor(x1[:, n, :], bank[k][:], x1[:, n, :], ALU.add).then_inc(x1_done, 1)

                def statistics(t):
                    v.wait_ge(x1_done, t + 1)
                    v.bn_stats(stats[:, t, :], x1[:, t, :]).then_inc(stats_done, 1)

                def variances(g):
                    half = slice(G8 * g, G8 * (g + 1))
                    for t in range(G8 * g, G8 * (g + 1)):
                        v.wait_ge(stats_done, t + 1)
                        v.bn_aggr(mv[:, t, :], stats[:, t, :]).then_inc(mv_done, 1)
                    v.wait_ge(mv_done, G8 * (g + 1))
                    v.tensor_scalar(var[:, half], mv[:, half, 1], EPS, None, ALU.add).then_inc(var_ready, 1)

                def norms(g):
                    half = slice(G8 * g, G8 * (g + 1))
                    v.wait_ge(ln_root, g + 1)
                    refine_rsqrt(v, ln_chain, 5 * g, var[:, half], root[:, half], rstd[:, half], tmp[:, half])
                    v.scalar_tensor_tensor(out=nmr[:, half], in0=mv[:, half, 0], scalar=-1.0,
                                           in1=rstd[:, half], op0=ALU.mult, op1=ALU.mult
                                           ).then_inc(norm_ready, 1)

                with v.Fori(0, T // SLOTS) as j:
                    for r in range(SLOTS):
                        cut(0, j, r)
                cut(1, 0, 0)
                v.wait_ge(x_loaded, 16)
                add_y(0)
                for s in range(1, 2 * SLOTS):
                    cut(1, s // SLOTS, s % SLOTS)
                    if s <= G8 // 2:
                        statistics(2 * s - 2)
                        statistics(2 * s - 1)
                variances(0)
                v.wait_ge(w_loaded, 16 * (KC + 2))
                w_rows = w_f[:].rearrange("p k h d -> p k (h d)")
                v.tensor_copy(w_hi[:], w_rows).then_inc(w_chain, 1)
                for r in range(SLOTS):
                    cut(1, 2, r)
                    if r == 0:
                        v.wait_ge(w_chain, 1)
                        v.tensor_tensor(w_lo[:], w_rows, w_hi[:].bitcast(F32), ALU.subtract).then_inc(w_ready, 1)
                norms(0)
                for r in range(SLOTS):
                    cut(1, 3, r)
                add_y(1)

                def cut_turned(t, b):
                    v.wait_ge(t_hi_ready, t + 1)
                    v.tensor_tensor(g_lo[:, b, :], bank[b][:], g_hi[:, b, :].bitcast(F32),
                                    ALU.subtract).then_inc(t_lo_ready, 1)

                def reduce_e(t, b):
                    for n in range(2):
                        v.wait_ge(prod_ready, 2 * t + n + 2)
                        v.tensor_reduce(e[:, t, n * H:(n + 1) * H], per_head(prod[:, b, n, :]),
                                        AX_X, ALU.add).then_inc(e_ready, 1)

                def more_statistics(k, b):
                    statistics(2 * k + G8)
                    statistics(2 * k + G8 + 1)

                def second_norms():
                    variances(1)
                    norms(1)

                v.sem_inc(e_ready, 4)
                skewed(v, T, ((cut_turned, 0), (more_statistics, 0, G8 // 2), (reduce_e, 2, T - 1)),
                       (G8 // 2, second_norms))

                def take_e_t(q):
                    v.wait_ge(e_turned, q + 1)
                    v.tensor_copy(e_t[:, q * 512:(q + 1) * 512], bank[4 + q][0:2 * H, :]).then_inc(e_copied, 1)
                    v.tensor_reduce(tops[:, q:q + 1], bank[4 + q][0:2 * H, :], AX_X, ALU.max).then_inc(top_ready, 1)

                for q in range(3):
                    take_e_t(q)
                reduce_e(T - 1, (T - 1) % 2)
                take_e_t(3)
                v.wait_ge(top_ready, 4)
                v.tensor_reduce(top[:], tops[:], AX_X, ALU.max).then_inc(top_ready, 1)
                v.wait_ge(top_ready, 5)
                v.tensor_copy(top_w[:], top[:].to_broadcast([2 * H, P])).then_inc(top_ready, 1)
                v.wait_ge(top_spread, 1)
                v.tensor_copy(dst_top[:, 0, :], bank[0][:, H:2 * H]).then_inc(top_ready, 1)

            @block.tensor
            def _(pe):
                pe.sem_inc(slot_free, 2)

                def products(s, b, g, first, last):
                    pe.wait_ge(g_ready, s + 1)
                    pe.wait_ge(lo_ready, s + 1)
                    for k in range(G8):
                        if first and g == 1:
                            pe.wait_ge(x1_done, k + 1)
                        cols = slice(k * P, (k + 1) * P)
                        mm = split_product(pe, bank[k][:], a_hi[:, b, cols], a_lo[:, b, cols],
                                           g_hi[:, b, :], g_lo[:, b, :], first)
                        if last:
                            mm.then_inc(acc_done, 1)
                    if not last:
                        mm.then_inc(slot_free, 1)

                for g in range(2):
                    products(T * g, 0, g, True, False)
                    with pe.Fori(0, T // 2 - 1) as j:
                        products(T * g + 2 * j + 1, 1, g, False, False)
                        products(T * g + 2 * j + 2, 0, g, False, False)
                    products(T * g + T - 1, 1, g, False, True)
                    if g == 0:
                        pe.wait_ge(acc_done, G8)
                        pe.sem_inc(slot_free, 1)

                def turn(t, b):
                    pe.wait_ge(h_ready, t + 1)
                    for k in range(KC):
                        cols = slice(k * P, (k + 1) * P)
                        mm = pe.transpose(bank[b][:, cols], h2[:, b, cols], ident[:])
                    mm.then_inc(turned, 1)

                def project(t, b):
                    pe.wait_ge(t_lo_ready, t + 1)
                    pe.wait_ge(wh_ready, t + 1)
                    for k in range(KC):
                        cols = slice(k * P, (k + 1) * P)
                        mm = split_product(pe, bank[2 + b][:], g_hi[:, b, cols], g_lo[:, b, cols],
                                           w_hi[:, k, :], w_lo[:, k, :], k == 0)
                    mm.then_inc(wh_summed, 1)

                pe.wait_ge(x1_done, G8 + 4)
                pe.wait_ge(w_ready, 1)
                pe.sem_inc(turned, 2)
                pe.sem_inc(wh_summed, 2)
                skewed(pe, T, ((turn, 0), (project, 1)))
                for t in range(T):
                    if t % 4 == 0:
                        pe.wait_ge(e_ready, 2 * t + 8 + 4)
                    mm = pe.transpose(bank[4 + t // 4][0:2 * H, (t % 4) * P:(t % 4 + 1) * P], e[:, t, :], ident[:])
                    if t % 4 == 3:
                        mm.then_inc(e_turned, 1)
                pe.wait_ge(top_ready, 6)
                pe.matmul(bank[0][:, 0:2 * H], top_w[:], ident[0:2 * H, 0:2 * H], start=True, stop=True
                          ).then_inc(top_spread, 1)


def attend(nc, bank, wh, e, mask, e_rows, dst_top, wh_store):
    with ExitStack() as ctx:
        def sb(name, shape, dt=F32):
            return ctx.enter_context(nc.sbuf_tensor(name, shape, dt))

        def sem(name):
            return ctx.enter_context(nc.semaphore(name))

        GT = 4
        QW = GT * P
        QUAD = 4
        NQ = T // QUAD
        PW = 4 * HE
        A_HI, C_HI, C_LO, A_LO = (slice(k * HE, (k + 1) * HE) for k in range(4))
        BOTH_C = slice(HE, 3 * HE)
        fac = {f: sb(f"fac_{f}", [P, T, H]) for f in "ABCD"}
        neg_d = sb("l4_neg_d", [P, T, H])
        args = [sb(f"l4_args{k}", [P, T, H]) for k in range(3)]
        src = sb("l4_src", [P, 2, 2, QW])
        q = sb("l4_q", [P, 2 * QUAD, QW], F32R)
        m_r = sb("l4_mask", [P, 2 * QUAD, QW], F32R)
        parts = sb("l4_parts", [P, 2, 2, T, PW], F32R)
        whole = sb("l4_whole", [P, T, HE])
        o = sb("l4_o", [P, 2, 3, GT, PW])
        first_whole = o[:].rearrange("p a b c d -> p (a b c d)")[:, 0:4 * T * HE].rearrange(
            "p (k t e) -> p k t e", k=4, t=T)

        wh_stored = sem("l4_wh_stored")
        chain = sem("l4_chain")
        args_ready = sem("l4_args_ready")
        fac_ready = sem("l4_fac_ready")
        src_loaded = [sem(f"l4_src_loaded{b}") for b in range(2)]
        first_whole_ready = sem("l4_first_whole_ready")
        first_hi = sem("l4_first_hi")
        first_lo = sem("l4_first_lo")
        second_whole_ready = sem("l4_second_whole_ready")
        second_hi = sem("l4_second_hi")
        second_lo = sem("l4_second_lo")
        whole_ready = sem("l4_whole_ready")
        part_hi = sem("l4_part_hi")
        part_lo = sem("l4_part_lo")
        q_ready = sem("l4_q_ready")
        q_done = sem("l4_q_done")
        m_ready = sem("l4_m_ready")
        m_done = sem("l4_m_done")
        q_bank_free = sem("l4_q_bank_free")
        m_bank_free = sem("l4_m_bank_free")
        scaled = sem("l4_scaled")
        o_free = sem("l4_o_free")
        held = sem("l4_held")
        SRC_EARLY = 2 * 2 * T
        AHEAD = 2 * GT
        LAST = 4 * (H // 2) - 1
        STEPS = 6

        def rounds(eng, hp, body):
            with eng.Fori(0, 2) as k:
                for b in range(2):
                    body(4 * hp + 2 * k + b, k, b)

        def combine(eng, r, tiles, b, hp):
            two = slice(2 * hp, 2 * hp + 2)
            over_q = o[:, b, 0:2, :, :].rearrange("p h t e -> p t h e")
            over_m = o[:, b, 2, :, :].rearrange("p t (h e) -> p t h e", h=2)
            a_sum, c_sum, m_sum = over_q[:, :, :, A_HI], over_q[:, :, :, C_HI], over_m[:, :, :, 0:HE]

            def step(n, out, in0, in1, op):
                if n:
                    eng.wait_ge(scaled, STEPS * r + n)
                    eng.sem_inc(held, 1)
                eng.tensor_tensor(out, in0, in1, op).then_inc(scaled, 1)

            def factor(f):
                return fac[f][:, tiles, two].unsqueeze(3).to_broadcast([P, GT, 2, HE])

            eng.wait_ge(q_bank_free, GT * (2 * r + 3))
            step(0, a_sum, a_sum, over_q[:, :, :, A_LO], ALU.add)
            step(1, a_sum, a_sum, factor("B"), ALU.mult)
            step(2, c_sum, c_sum, over_q[:, :, :, C_LO], ALU.add)
            eng.wait_ge(m_bank_free, GT * (r + 2))
            step(3, m_sum, m_sum, over_m[:, :, :, HE:2 * HE], ALU.add)
            step(4, m_sum, m_sum, c_sum, ALU.subtract)
            step(5, m_sum, m_sum, factor("D"), ALU.mult)
            eng.wait_ge(scaled, STEPS * r + 6)
            eng.sem_inc(held, 1)
            eng.tensor_tensor(wh[:, tiles, two, :], a_sum, m_sum, ALU.add).then_inc(o_free, 1)

        with nc.Block() as block:
            @block.sync
            def _(sp):
                for hp in range(H // 2):
                    def load(r, k, b, hp=hp):
                        sp.wait_ge(q_ready, 2 * T * r + 2 * T)
                        for hh in range(2):
                            row = e_rows[2 * hp + hh:2 * hp + hh + 1, bass.ds(2 * QW * k + QW * b, QW)]
                            sp.dma_start(src[:, b, hh, :], row.to_broadcast([P, QW])).then_inc(src_loaded[b], 16)
                    rounds(sp, hp, load)

            @block.vector
            def _(v):
                v.sem_inc(q_ready, SRC_EARLY)
                s_n, d_m = e[:, :, 0:H], e[:, :, H:2 * H]
                top_t = dst_top[:].to_broadcast([P, T, H])
                v.tensor_tensor(args[0][:], d_m, top_t, ALU.subtract).then_inc(args_ready, 1)
                v.tensor_tensor(args[1][:], s_n, top_t, ALU.add).then_inc(chain, 1)
                v.tensor_scalar(neg_d[:], d_m, -1.0, None, ALU.mult).then_inc(chain, 1)
                v.wait_ge(chain, 2)
                v.tensor_scalar(args[2][:], args[1][:], 1.0 - SLOPE, 0.0, ALU.mult, ALU.min).then_inc(args_ready, 1)
                v.wait_ge(args_ready, 2)
                v.tensor_scalar(args[1][:], args[1][:], SLOPE - 1.0, 0.0, ALU.mult, ALU.min).then_inc(args_ready, 1)
                for n in range(2):
                    v.wait_ge(fac_ready, n + 1)
                    v.tensor_tensor(first_whole[:, n, :, :], wh[:, :, 0, :],
                                    fac["AC"[n]][:, :, 0:1].to_broadcast([P, T, HE]),
                                    ALU.mult).then_inc(first_whole_ready, 1)
                for n in range(2):
                    v.wait_ge(first_hi, n + 1)
                    v.tensor_tensor(parts[:, 0, 0, :, (A_LO, C_LO)[n]], first_whole[:, n, :, :],
                                    parts[:, 0, 0, :, (A_HI, C_HI)[n]].bitcast(F32),
                                    ALU.subtract).then_inc(first_lo, 1)

                for hp in range(H // 2):
                    def choose(r, k, b, hp=hp):
                        cols = bass.ds(2 * QW * k + QW * b, QW)
                        for hh in range(2):
                            h = 2 * hp + hh
                            for i in range(T):
                                if (i // QUAD + 2) % NQ != NQ - 1:
                                    v.wait_ge(q_done, QUAD * (2 * NQ * r + NQ * hh) + i + 1)
                                elif i % QUAD == 0:
                                    v.wait_ge(q_done, QUAD * (2 * NQ * r + NQ * hh) + i + QUAD)
                                if i == 0 and hh == 0:
                                    v.wait_ge(src_loaded[b], 32 * (2 * hp + k) + 32)
                                v.scalar_tensor_tensor(out=q[:, i % (2 * QUAD), :], in0=src[:, b, hh, :],
                                                       scalar=neg_d[:, i, h:h + 1], in1=mask[:, i, cols],
                                                       op0=ALU.is_ge, op1=ALU.mult).then_inc(q_ready, 1)
                    rounds(v, hp, choose)
                v.wait_ge(o_free, 2 + LAST)
                combine(v, LAST, slice(T - GT, T), LAST % 2, H // 2 - 1)

            @block.scalar
            def _(a):
                a.sem_inc(q_bank_free, GT)
                a.sem_inc(m_bank_free, GT)

                def take_mask(r, quad, cols):
                    a.wait_ge(m_done, GT * (NQ * r + quad + 1))
                    for i in range(QUAD):
                        a.activation(m_r[:, quad % 2 * QUAD + i, :], mask[:, QUAD * quad + i, cols],
                                     ACT.Copy).then_inc(m_ready, 1)

                def take_q_sums(r, b, hh):
                    for t in range(GT):
                        a.wait_ge(q_done, AHEAD + GT * (2 * NQ * r + NQ * hh + NQ - 1) + t + 1)
                        a.activation(o[:, b, hh, t, :], bank[t][:, 0:PW], ACT.Copy).then_inc(q_bank_free, 1)

                a.wait_ge(args_ready, 1)
                a.activation(fac["A"][:], args[0][:], ACT.Exp).then_inc(fac_ready, 1)
                a.activation(fac["C"][:], args[0][:], ACT.Exp, scale=SLOPE).then_inc(fac_ready, 1)
                a.wait_ge(args_ready, 2)
                a.activation(fac["B"][:], args[2][:], ACT.Exp).then_inc(fac_ready, 1)
                a.wait_ge(args_ready, 3)
                a.activation(fac["D"][:], args[1][:], ACT.Exp).then_inc(fac_ready, 1)
                for n in range(2):
                    a.wait_ge(first_whole_ready, n + 1)
                    a.activation(parts[:, 0, 0, :, (A_HI, C_HI)[n]], first_whole[:, n, :, :],
                                 ACT.Copy).then_inc(first_hi, 1)
                take_mask(0, 0, slice(0, QW))
                for n in range(2):
                    a.wait_ge(second_whole_ready, n + 1)
                    a.activation(parts[:, 0, 1, :, (C_HI, A_HI)[n]], first_whole[:, 2 + n, :, :],
                                 ACT.Copy).then_inc(second_hi, 1)
                take_mask(0, 1, slice(0, QW))
                for hp in range(H // 2):
                    def serve(r, k, b, hp=hp):
                        cols = bass.ds(2 * QW * k + QW * b, QW)
                        after = bass.ds(2 * QW * k + QW, QW) if b == 0 else bass.ds(2 * QW - 2 * QW * k, QW)
                        take_mask(r, 2, cols)
                        a.wait_ge(o_free, r + 1)
                        take_q_sums(r, b, 0)
                        take_mask(r, 3, cols)
                        if hp + 1 < H // 2:
                            a.wait_ge(whole_ready, r + 1)
                            a.sem_inc(held, 1)
                            a.activation(parts[:, (hp + 1) % 2, k, :, (A_HI, C_HI)[b]], whole[:], ACT.Copy
                                         ).then_inc(part_hi, 1)
                        take_mask(r + 1, 0, after)
                        take_q_sums(r, b, 1)
                        for t in range(GT):
                            a.wait_ge(m_done, AHEAD + GT * (NQ * r + NQ - 1) + t + 1)
                            a.activation(o[:, b, 2, t, :], bank[GT + t][:, 0:PW], ACT.Copy).then_inc(m_bank_free, 1)
                        take_mask(r + 1, 1, after)
                    rounds(a, hp, serve)

            @block.gpsimd
            def _(p):
                p.sem_inc(o_free, 2)
                p.sem_inc(part_lo, 1)
                for n in range(2):
                    p.wait_ge(fac_ready, 2)
                    p.tensor_tensor(first_whole[:, 2 + n, :, :], wh[:, :, 1, :],
                                    fac["CA"[n]][:, :, 1:2].to_broadcast([P, T, HE]),
                                    ALU.mult).then_inc(second_whole_ready, 1)
                for n in range(2):
                    p.wait_ge(second_hi, n + 1)
                    p.tensor_tensor(parts[:, 0, 1, :, (C_LO, A_LO)[n]], first_whole[:, 2 + n, :, :],
                                    parts[:, 0, 1, :, (C_HI, A_HI)[n]].bitcast(F32),
                                    ALU.subtract).then_inc(second_lo, 1)
                for b in range(2):
                    p.wait_ge(src_loaded[b], 32)
                p.dma_start(wh_store.rearrange("(t p) f -> p t f", p=P),
                            wh[:].rearrange("p t h e -> p t (h e)")).then_inc(wh_stored, 16)
                p.wait_ge(fac_ready, 4)
                for hp in range(H // 2):
                    def cut_and_combine(r, k, b, hp=hp):
                        if hp + 1 < H // 2:
                            head = bass.ds(2 * hp + 2 + k, 1)
                            p.wait_ge(part_lo, r + 1)
                            p.sem_inc(held, 1)
                            p.tensor_tensor(whole[:], wh[:, :, head, :].rearrange("p t o e -> p t (o e)"),
                                            fac["AC"[b]][:, :, head].to_broadcast([P, T, HE]),
                                            ALU.mult).then_inc(whole_ready, 1)
                            p.wait_ge(part_hi, r + 1)
                            p.sem_inc(held, 1)
                            part = parts[:, (hp + 1) % 2, k, :, :]
                            p.tensor_tensor(part[:, :, (A_LO, C_LO)[b]], whole[:],
                                            part[:, :, (A_HI, C_HI)[b]].bitcast(F32),
                                            ALU.subtract).then_inc(part_lo, 1)

                        if hp == 0:
                            p.wait_ge(wh_stored, 16)
                        if hp + 1 < H // 2:
                            combine(p, r, bass.ds(2 * GT * k + GT * b, GT), b, hp)
                        elif r < LAST:
                            combine(p, r, slice(2 * GT * k + GT * b, 2 * GT * k + GT * (b + 1)), b, hp)
                    if hp + 1 < H // 2:
                        rounds(p, hp, cut_and_combine)
                    else:
                        for n in range(4):
                            cut_and_combine(4 * hp + n, n // 2, n % 2)

            @block.tensor
            def _(pe):
                pe.sem_inc(q_done, AHEAD)
                pe.sem_inc(m_done, AHEAD)

                def q_quad(r, pair_slot, hh, quad):
                    made = SRC_EARLY + 2 * T * r + T * hh + QUAD * quad

                    def product(t, i):
                        return pe.matmul(bank[t][:, 0:PW], q[:, i % (2 * QUAD), t * P:(t + 1) * P],
                                         parts[:, pair_slot, hh, i, :], start=i == 0, stop=i == T - 1,
                                         skip_group_check=True)

                    if quad < NQ - 1:
                        for i in range(QUAD * quad, QUAD * (quad + 1)):
                            pe.wait_ge(q_ready, made + i % QUAD + 1)
                            for t in range(GT):
                                if i == 0:
                                    pe.wait_ge(q_bank_free, GT * (2 * r + hh) + t + 1)
                                mm = product(t, i)
                            mm.then_inc(q_done, 1)
                    else:
                        pe.wait_ge(q_ready, made + QUAD)
                        for t in range(GT):
                            for i in range(QUAD * quad, T):
                                mm = product(t, i)
                            mm.then_inc(q_done, 1)

                def m_quad(r, pair_slot, quad):
                    pe.wait_ge(m_ready, GT * (NQ * r + quad) + GT)
                    for t in range(GT):
                        if quad == 0:
                            pe.wait_ge(m_bank_free, GT * r + t + 1)
                        for b in range(QUAD):
                            i = QUAD * quad + b
                            mm = pe.matmul(bank[GT + t][:, 0:PW], m_r[:, i % (2 * QUAD), t * P:(t + 1) * P],
                                           parts[:, pair_slot, :, i, BOTH_C], start=i == 0, stop=i == T - 1,
                                           skip_group_check=True)
                        mm.then_inc(m_done, 1)

                pe.wait_ge(first_lo, 2)
                with pe.Fori(0, H // 4) as j:
                    for pair_slot in range(2):
                        hp = 2 * j + pair_slot

                        def sum_up(r, k, b):
                            pe.wait_ge(part_lo, 4 * hp + 1)
                            for hh in range(2):
                                if hh:
                                    pe.wait_ge(second_lo, 2)
                                for half in range(2):
                                    q_quad(r, pair_slot, hh, 2 * half)
                                    q_quad(r, pair_slot, hh, 2 * half + 1)
                                    if hh == 0 and half == 0:
                                        pe.wait_ge(second_lo, 1)
                                    m_quad(r, pair_slot, 2 * hh + half)
                        rounds(pe, hp, sum_up)


def attend_exactly(nc, bank, wh, e, ident, retry, adj, e_rows, wh_store):
    NEG = -9e15
    with ExitStack() as ctx:
        def sb(name, shape, dt=F32):
            return ctx.enter_context(nc.sbuf_tensor(name, shape, dt))

        def sem(name):
            return ctx.enter_context(nc.semaphore(name))

        rows = sb("l6_rows", [P, N])
        shut = sb("l6_shut", [P, N])
        dst = sb("l6_dst", [P, N])
        z = sb("l6_z", [P, N])
        probs = sb("l6_probs", [P, N])
        probs_t = sb("l6_probs_t", [P, T, P])
        top = sb("l6_top", [P, 1])
        sums = sb("l6_sums", [P, T, H, HE])

        wh_loaded = sem("l6_wh_loaded")
        rows_loaded = sem("l6_rows_loaded")
        dst_loaded = sem("l6_dst_loaded")
        masked = sem("l6_masked")
        scored = sem("l6_scored")
        exp_done = sem("l6_exp_done")
        turned = sem("l6_turned")
        copied = sem("l6_copied")
        summed = sem("l6_summed")
        kept = sem("l6_kept")

        def units(eng, body):
            with eng.Fori(0, T) as t:
                for h in range(H):
                    body(t, H * t + h, h)

        with nc.Block() as block:
            @block.sync
            def _(sp):
                with if_set(sp, retry):
                    sp.dma_start(wh[:].rearrange("p t h e -> p t (h e)"),
                                 wh_store.rearrange("(t p) f -> p t f", p=P)).then_inc(wh_loaded, 16)

                    def load(t, unit, h):
                        sp.wait_ge(kept, unit + 1)
                        if h == 0:
                            sp.dma_start(rows[:], adj[bass.ds(t * P, P), :]).then_inc(rows_loaded, 16)
                        sp.dma_start(dst[:], e_rows[H + h:H + h + 1, :].to_broadcast([P, N])).then_inc(dst_loaded, 16)
                    units(sp, load)

            @block.vector
            def _(v):
                with if_set(v, retry):
                    v.sem_inc(kept, 1)

                    def score(t, unit, h):
                        if h == 0:
                            v.wait_ge(rows_loaded, 16 * t + 16)
                            v.tensor_scalar(rows[:], rows[:], 0.0, None, ALU.is_gt).then_inc(masked, 1)
                            v.wait_ge(masked, 2 * t + 1)
                            v.tensor_scalar(shut[:], rows[:], -NEG, NEG, ALU.mult, ALU.add).then_inc(masked, 1)
                            v.wait_ge(masked, 2 * t + 2)
                        v.wait_ge(dst_loaded, 16 * unit + 16)
                        v.tensor_scalar(z[:], dst[:], e[:, bass.ds(t, 1), h], None, ALU.add).then_inc(scored, 1)
                        v.wait_ge(scored, 6 * unit + 1)
                        v.scalar_tensor_tensor(out=z[:], in0=z[:], scalar=SLOPE, in1=z[:], op0=ALU.mult,
                                               op1=ALU.max).then_inc(scored, 1)
                        v.wait_ge(scored, 6 * unit + 2)
                        v.tensor_tensor(z[:], z[:], rows[:], ALU.mult).then_inc(scored, 1)
                        v.wait_ge(scored, 6 * unit + 3)
                        v.tensor_tensor(z[:], z[:], shut[:], ALU.add).then_inc(scored, 1)
                        v.wait_ge(scored, 6 * unit + 4)
                        v.tensor_reduce(top[:], z[:], AX_X, ALU.max).then_inc(scored, 1)
                        v.wait_ge(scored, 6 * unit + 5)
                        v.tensor_scalar(z[:], z[:], top[:], None, ALU.subtract).then_inc(scored, 1)
                        for k in range(4):
                            v.wait_ge(turned, 4 * unit + k + 1)
                            v.tensor_copy(probs_t[:, 4 * k:4 * k + 4, :].rearrange("p t n -> p (t n)"),
                                          bank[k][:]).then_inc(copied, 1)
                        v.wait_ge(summed, unit + 1)
                        v.tensor_copy(sums[:, bass.ds(t, 1), h, :].rearrange("p o e -> p (o e)"),
                                      bank[4][:, 0:HE]).then_inc(kept, 1)
                    units(v, score)
                    v.wait_ge(kept, T * H + 1)
                    v.tensor_copy(wh[:], sums[:]).then_inc(masked, 1)

            @block.scalar
            def _(a):
                with if_set(a, retry):
                    def exp(t, unit, h):
                        a.wait_ge(scored, 6 * unit + 6)
                        a.activation(probs[:], z[:], ACT.Exp).then_inc(exp_done, 1)
                    units(a, exp)

            @block.tensor
            def _(pe):
                with if_set(pe, retry):
                    pe.wait_ge(wh_loaded, 16)

                    def average(t, unit, h):
                        pe.wait_ge(exp_done, unit + 1)
                        for k in range(4):
                            for b in range(4):
                                m = 4 * k + b
                                mm = pe.transpose(bank[k][:, b * P:(b + 1) * P], probs[:, m * P:(m + 1) * P], ident[:])
                            mm.then_inc(turned, 1)
                        pe.wait_ge(copied, 4 * unit + 4)
                        for m in range(T):
                            mm = pe.matmul(bank[4][:, 0:HE], probs_t[:, m, :], wh[:, m, h, :], start=m == 0,
                                           stop=m == T - 1)
                        mm.then_inc(summed, 1)
                    units(pe, average)


def feed_forward(nc, bank, wh, ident, retry, again, x1_store, w1_t, b1, w2_t, b2, w3_t, b3, w4_t, b4, out):
    tag = "l7" if again else "l5"
    only_if = retry if again else None
    F1, F2, F3 = w1_t.shape[1], w2_t.shape[1], w3_t.shape[1]
    K1, K3 = F1 // P, F3 // P
    TC = 4
    CW = TC * P
    with ExitStack() as ctx:
        def sb(name, shape, dt=F32):
            return ctx.enter_context(nc.sbuf_tensor(name, shape, dt))

        def sem(name):
            return ctx.enter_context(nc.semaphore(name))

        w1_s = sb(f"{tag}_w1", [P, KC, F1])
        w2_s = sb(f"{tag}_w2", [P, K1, F2])
        w3_s = sb(f"{tag}_w3", [P, F3])
        w4_s = sb(f"{tag}_w4", [P, K3, F])
        b1_s = sb(f"{tag}_b1", [P, K1])
        b2_s = sb(f"{tag}_b2", [P, 1])
        b3_s = sb(f"{tag}_b3", [P, K3])
        b4_s = sb(f"{tag}_b4", [P, 1, F])
        share = sb(f"{tag}_share", [P, T * H, 1])
        ones = sb(f"{tag}_ones", [P, 1])
        fine = sb(f"{tag}_fine", [P, T * H, 1])
        fine_sum = sb(f"{tag}_fine_sum", [P, 1])
        neg = sb(f"{tag}_neg", [P, TC * H, HD])
        enc = sb(f"{tag}_enc", [P, TC, F])
        w1_hi = sb(f"{tag}_w1_hi", [P, KC, F1], F32R)
        w1_lo = sb(f"{tag}_w1_lo", [P, KC, F1], F32R)
        enc_t_hi = sb(f"{tag}_enc_t_hi", [P, 2, KC, CW], F32R)
        enc_t_lo = sb(f"{tag}_enc_t_lo", [P, 2, KC, CW], F32R)
        o1 = sb(f"{tag}_o1", [P, K1, CW])
        o2 = sb(f"{tag}_o2", [P, CW])
        o3 = sb(f"{tag}_o3", [P, K3, CW])
        res = sb(f"{tag}_res", [P, 2, TC, F])
        ROW_BANKS = (7, 4)

        w_loaded = sem(f"{tag}_w_loaded")
        x_loaded = [sem(f"{tag}_x_loaded{b}") for b in range(2)]
        retry_chain = sem(f"{tag}_retry_chain")
        fine_counted = sem(f"{tag}_fine_counted")
        share_ready = sem(f"{tag}_share_ready")
        averaged = sem(f"{tag}_averaged")
        neg_ready = sem(f"{tag}_neg_ready")
        exp_ready = sem(f"{tag}_exp_ready")
        pos_ready = sem(f"{tag}_pos_ready")
        enc_ready = sem(f"{tag}_enc_ready")
        turned = sem(f"{tag}_turned")
        w1_hi_ready = sem(f"{tag}_w1_hi_ready")
        w1_lo_ready = sem(f"{tag}_w1_lo_ready")
        enc_t_hi_ready = sem(f"{tag}_enc_t_hi_ready")
        enc_t_ready = sem(f"{tag}_enc_t_ready")
        sums_done = sem(f"{tag}_sums_done")
        act_ready = sem(f"{tag}_act_ready")
        biased = sem(f"{tag}_biased")
        rows_done = sem(f"{tag}_rows_done")
        out_ready = sem(f"{tag}_out_ready")
        stored = [sem(f"{tag}_stored{b}") for b in range(2)]
        last_stored = [sem(f"{tag}_last_stored{t}") for t in range(TC)]
        zs = wh[:].rearrange("p t h e -> p (t h) e")
        NCH = T // TC

        with nc.Block() as block:
            @block.sync
            def _(sp):
                with if_set(sp, only_if):
                    for dst, src in ((w1_s, w1_t.rearrange("(k p) f -> p k f", p=P)),
                                     (b1_s, b1), (b2_s, b2), (b3_s, b3),
                                     (w2_s, w2_t.rearrange("(k p) f -> p k f", p=P)),
                                     (w3_s, w3_t), (w4_s, w4_t.rearrange("(k p) f -> p k f", p=P))):
                        sp.dma_start(dst[:], src).then_inc(w_loaded, 16)
                    sp.dma_start(b4_s[:, 0, :], b4.rearrange("(o f) -> o f", o=1).to_broadcast([P, F])
                                 ).then_inc(w_loaded, 16)

                    def rows(c):
                        return bass.ds(c * CW, CW)

                    def load(c, b):
                        if c >= 2:
                            sp.wait_ge(stored[b], 16 * (c // 2))
                        sp.dma_start(res[:, b, :, :], x1_store[rows(c), :].rearrange("(t p) f -> p t f", p=P)
                                     ).then_inc(x_loaded[b], 16)

                    def store(c, b):
                        step = 1 if c == NCH - 1 else TC
                        for t in range(0, TC, step):
                            sp.wait_ge(out_ready, TC * c + t + step + 2)
                            done = sp.dma_start(out[(c * TC + t) * P:(c * TC + t + step) * P, :].rearrange(
                                "(t p) f -> p t f", p=P), res[:, b, t:t + step, :])
                            done.then_inc(last_stored[t] if step == 1 else stored[b], 16)

                    for k in range(NCH + 1):
                        if k < NCH:
                            load(k, k % 2)
                        if k:
                            store(k - 1, (k - 1) % 2)
                    for b in range(2):
                        sp.wait_ge(stored[b], 16 * ((NCH - b) // 2))
                    for t in range(TC):
                        sp.wait_ge(last_stored[t], 16)

            @block.vector
            def _(v):
                with if_set(v, only_if):
                    enc_z = enc[:].rearrange("p t (h d) -> p (t h) d", h=H)
                    v.tensor_scalar(share[:], zs[:, :, HD:HE], TINY, None, ALU.max).then_inc(share_ready, 1)
                    v.wait_ge(share_ready, 1)
                    v.reciprocal(share[:], share[:]).then_inc(share_ready, 1)
                    v.wait_ge(share_ready, 2)

                    def elu(c):
                        halves = [slice((2 * c + k) * TC * H // 2, (2 * c + k + 1) * TC * H // 2) for k in range(2)]
                        here = [slice(k * TC * H // 2, (k + 1) * TC * H // 2) for k in range(2)]
                        for k in range(2):
                            z = zs[:, halves[k], 0:HD]
                            v.tensor_tensor(z, z, share[:, halves[k], :].to_broadcast([P, TC * H // 2, HD]),
                                            ALU.mult).then_inc(averaged, 1)
                            v.wait_ge(averaged, 2 * c + k + 1)
                            if c:
                                v.wait_ge(enc_ready, 2 * c - 1 + k)
                            v.tensor_scalar(neg[:, here[k], :], z, 0.0, None, ALU.min).then_inc(neg_ready, 1)
                        if c:
                            v.wait_ge(turned, KC * c)
                        for k in range(2):
                            v.tensor_scalar(enc_z[:, here[k], :], zs[:, halves[k], 0:HD], 0.0, -1.0, ALU.max,
                                            ALU.add).then_inc(pos_ready, 1)
                        for k in range(2):
                            v.wait_ge(exp_ready, 2 * c + k + 1)
                            v.wait_ge(pos_ready, 2 * c + k + 1)
                            v.tensor_tensor(enc_z[:, here[k], :], enc_z[:, here[k], :], neg[:, here[k], :],
                                            ALU.add).then_inc(enc_ready, 1)

                    def take_turned(c, ks):
                        for k in ks:
                            v.wait_ge(enc_t_hi_ready, KC * c + k + 1)
                            v.tensor_tensor(enc_t_lo[:, c % 2, k, :], bank[k % 2][:],
                                            enc_t_hi[:, c % 2, k, :].bitcast(F32), ALU.subtract
                                            ).then_inc(enc_t_ready, 1)

                    def finish(c):
                        b = c % 2
                        for t in range(TC):
                            v.wait_ge(rows_done, TC * c + t + 1)
                            v.tensor_tensor(res[:, b, t, :], bank[ROW_BANKS[t % 2]][:], res[:, b, t, :], ALU.add
                                            ).then_inc(out_ready, 1)

                    v.sem_inc(out_ready, 2)
                    elu(0)
                    if not again:
                        v.memset(ones[:], 1.0).then_inc(retry_chain, 1)
                        v.tensor_scalar(fine[:], zs[:, :, HD:HE], LEAST_SUM, None, ALU.is_ge).then_inc(retry_chain, 1)
                        v.wait_ge(retry_chain, 2)
                        v.tensor_reduce(fine_sum[:], fine[:].rearrange("p n o -> p (n o)"), AX_X, ALU.add
                                        ).then_inc(retry_chain, 1)
                    take_turned(0, range(KC))
                    v.wait_ge(w_loaded, 16 * 8)
                    for c in range(NCH):
                        if c + 1 < NCH:
                            elu(c + 1)
                        v.wait_ge(x_loaded[c % 2], 16 * (c // 2) + 16)
                        v.tensor_tensor(res[:, c % 2, :, :], res[:, c % 2, :, :], b4_s[:].to_broadcast([P, TC, F]),
                                        ALU.add).then_inc(biased, 1)
                        v.wait_ge(biased, c + 1)
                        if c + 1 < NCH:
                            take_turned(c + 1, range(KC))
                        if c == 0 and not again:
                            v.wait_ge(fine_counted, 1)
                            v.tensor_scalar(retry[:], bank[7][0:1, 0:1], float(P * T * H), None, ALU.not_equal
                                            ).then_inc(retry_chain, 1)
                        finish(c)

            @block.scalar
            def _(a):
                with if_set(a, only_if):
                    def exp(c):
                        for k in range(2):
                            half = neg[:, k * TC * H // 2:(k + 1) * TC * H // 2, :]
                            a.wait_ge(neg_ready, 2 * c + k + 1)
                            a.activation(half, half, ACT.Exp).then_inc(exp_ready, 1)

                    def take_turned(c, ks):
                        if c >= 2:
                            a.wait_ge(sums_done, 5 * (c - 2) + K1)
                        for k in ks:
                            a.wait_ge(turned, KC * c + k + 1)
                            a.activation(enc_t_hi[:, c % 2, k, :], bank[k % 2][:], ACT.Copy
                                         ).then_inc(enc_t_hi_ready, 1)

                    exp(0)
                    take_turned(0, range(0, 2))
                    a.wait_ge(w_loaded, 16 * 8)
                    a.activation(w1_hi[:], w1_s[:], ACT.Copy).then_inc(w1_hi_ready, 1)
                    take_turned(0, range(2, KC))
                    for c in range(NCH):
                        more = c + 1 < NCH
                        if more:
                            exp(c + 1)
                        for k in range(K1):
                            a.wait_ge(sums_done, 5 * c + k + 1)
                            a.activation(o1[:, k, :], bank[2 + k][:], ACT.Relu, bias=b1_s[:, k:k + 1]
                                         ).then_inc(act_ready, 1)
                        a.wait_ge(sums_done, 5 * c + 3)
                        a.activation(o2[:], bank[4][:], ACT.Relu, bias=b2_s[:, 0:1]).then_inc(act_ready, 1)
                        if more:
                            take_turned(c + 1, range(0, 2))
                        for k in range(K3):
                            a.wait_ge(sums_done, 5 * c + 4 + k)
                            a.activation(o3[:, k, :], bank[5 + k][:], ACT.Relu, bias=b3_s[:, k:k + 1]
                                         ).then_inc(act_ready, 1)
                        if more:
                            take_turned(c + 1, range(2, KC))

            @block.gpsimd
            def _(p):
                with if_set(p, only_if):
                    p.wait_ge(w1_hi_ready, 1)
                    p.tensor_tensor(w1_lo[:], w1_s[:], w1_hi[:].bitcast(F32), ALU.subtract
                                    ).then_inc(w1_lo_ready, 1)

            @block.tensor
            def _(pe):
                with if_set(pe, only_if):
                    def turn(c, ks):
                        pe.wait_ge(enc_ready, 2 * c + 2)
                        for k in ks:
                            if KC * c + k >= 2:
                                pe.wait_ge(enc_t_ready, KC * c + k - 1)
                            for t in range(TC):
                                mm = pe.transpose(bank[k % 2][:, t * P:(t + 1) * P], enc[:, t, k * P:(k + 1) * P],
                                                  ident[:])
                            mm.then_inc(turned, 1)

                    turn(0, range(KC))
                    if not again:
                        pe.wait_ge(retry_chain, 3)
                        pe.matmul(bank[7][0:1, 0:1], fine_sum[:], ones[:], start=True, stop=True
                                  ).then_inc(fine_counted, 1)
                    pe.wait_ge(w_loaded, 16 * 8)
                    pe.wait_ge(w1_lo_ready, 1)
                    for c in range(NCH):
                        more = c + 1 < NCH
                        pe.wait_ge(enc_t_ready, KC * c + KC)
                        for m in range(K1):
                            for k in range(KC):
                                rows_of = slice(m * P, (m + 1) * P)
                                mm = split_product(pe, bank[2 + m][:], w1_hi[:, k, rows_of], w1_lo[:, k, rows_of],
                                                   enc_t_hi[:, c % 2, k, :], enc_t_lo[:, c % 2, k, :], k == 0)
                            mm.then_inc(sums_done, 1)
                        pe.wait_ge(out_ready, TC * c + 2)
                        for k in range(K1):
                            pe.wait_ge(act_ready, 5 * c + k + 1)
                            mm = pe.matmul(bank[4][:], w2_s[:, k, :], o1[:, k, :], start=k == 0, stop=k == K1 - 1)
                        mm.then_inc(sums_done, 1)
                        if more:
                            turn(c + 1, range(0, 2))
                        pe.wait_ge(act_ready, 5 * c + 3)
                        for m in range(K3):
                            pe.matmul(bank[5 + m][:], w3_s[:, m * P:(m + 1) * P], o2[:], start=True, stop=True
                                      ).then_inc(sums_done, 1)
                        if more:
                            turn(c + 1, range(2, KC))
                        pe.wait_ge(act_ready, 5 * c + 5)
                        if c == 0 and not again:
                            pe.wait_ge(retry_chain, 4)
                        for t in range(TC):
                            pe.wait_ge(out_ready, TC * c + t + 1)
                            for k in range(K3):
                                mm = pe.matmul(bank[ROW_BANKS[t % 2]][:], o3[:, k, t * P:(t + 1) * P], w4_s[:, k, :],
                                               start=k == 0, stop=k == K3 - 1)
                            mm.then_inc(rows_done, 1)


def build(nc, x, adj, adj_t, w, a1, a2, w1_t, b1, w2_t, b2, w3_t, b3, w4_t, b4, out):
    e_rows = nc.dram_tensor("e_rows", (2 * H, N), F32, kind="Internal").ap()
    x1_store = nc.dram_tensor("x1_store", (N, F), F32, kind="Internal").ap()
    wh_store = nc.dram_tensor("wh_store", (N, H * HE), F32, kind="Internal").ap()
    with ExitStack() as ctx:
        def sb(name, shape, dt=F32, within=ctx):
            return within.enter_context(nc.sbuf_tensor(name, shape, dt))

        bank = [ctx.enter_context(nc.psum_tensor(f"bank{k}", [P, 512], F32)) for k in range(8)]
        ident = sb("ident", [P, P])
        make_identity(nc, ident)
        e = sb("e", [P, T, 2 * H])
        dst_top = sb("dst_top", [P, 1, H])
        smooth = ctx.enter_context(ExitStack())
        G = smooth.enter_context(nc.sbuf_tensor("G", [P, T, F], F32, side="right"))
        rows = smooth.enter_context(nc.sbuf_tensor("rows", [P, SLOTS, GW], F32, side="right"))
        rows_loaded = [smooth.enter_context(nc.semaphore(f"rows_loaded{r}")) for r in range(SLOTS)]
        smooth_features(nc, bank, G, rows, rows_loaded, x, adj, adj_t)
        mask = sb("mask", [P, T, N], U8)
        wh = sb("wh", [P, T, H, HE])
        with nc.sbuf_tensor("x1", [P, T, F], F32) as x1:
            spread_and_project(nc, bank, G, rows, rows_loaded, x1, mask, wh, e, ident, x, adj_t, w, a1, a2, e_rows,
                               dst_top, x1_store)
            smooth.close()
        attend(nc, bank, wh, e, mask, e_rows, dst_top, wh_store)
        retry = sb("retry", [1, 1], mybir.dt.int32)
        mlp = (w1_t, b1, w2_t, b2, w3_t, b3, w4_t, b4, out)
        feed_forward(nc, bank, wh, ident, retry, False, x1_store, *mlp)
        attend_exactly(nc, bank, wh, e, ident, retry, adj, e_rows, wh_store)
        feed_forward(nc, bank, wh, ident, retry, True, x1_store, *mlp)


_WEIGHTS = ("a1", "a2", "W1", "b1", "W2", "b2", "W3", "b3", "W4", "b4")


def kernel(x, adj, L1_gnn_W, **weights):
    import numpy as np
    import concourse.bacc as bacc
    from concourse.bass_utils import run_bass_kernel_spmd

    nc = bacc.Bacc("TRN2", target_bir_lowering=False, num_devices=1)
    arrays = {"x": x, "adj": adj, "adj_t": np.asarray(adj).T, "w": L1_gnn_W}
    for name in _WEIGHTS:
        a = np.asarray(weights[f"L1_gnn_{name}"])
        if name in ("b1", "b2", "b3"):
            a = a.reshape(-1, P)
        arrays[name] = a.T if a.ndim == 2 and name[0] != "a" else a
    arrays = {name: np.ascontiguousarray(a) for name, a in arrays.items()}
    aps = [nc.dram_tensor(name, a.shape, mybir.dt.from_np(a.dtype), kind="ExternalInput").ap()
           for name, a in arrays.items()]
    out = nc.dram_tensor("out", (N, F), F32, kind="ExternalOutput").ap()
    build(nc, *aps, out)
    return run_bass_kernel_spmd(nc, [arrays], core_ids=[0]).results[0]["out"]
```
